# Optimizing a Trainium2 kernel written in Bass

```python
import numpy as np
import jax
import jax.numpy as jnp

def _softmax(x, axis=-1):
    return jax.nn.softmax(x, axis=axis)

def _gelu(x):
    return jax.nn.gelu(x, approximate=True)

def _silu(x):
    return jax.nn.silu(x)

def _sigmoid(x):
    return jax.nn.sigmoid(x)

def _layernorm(x, axis=-1, eps=1e-05):
    m = jnp.mean(x, axis=axis, keepdims=True)
    v = jnp.var(x, axis=axis, keepdims=True)
    return (x - m) / jnp.sqrt(v + eps)

def _scatter_add(tgt, idx, src, axis=0):
    return tgt.at[idx].add(src)

def _segment_sum(src, seg, n):
    return jax.ops.segment_sum(src, seg, n)
kernel_name = 'mk_xattn_seq_d2_seqx_r2_369d7a'

def setup_inputs(seed: int=0):
    np.random.seed(seed)
    _w = jnp.asarray

    def _rec_inputs():
        import jax
        import jax.numpy as jnp
        _rk = jax.random.key(seed)
        x = 7.22e-05 + 1 * jax.random.normal(jax.random.fold_in(_rk, 1), (32, 256, 512), jnp.float32)
        _lenS = 256 - jax.random.randint(jax.random.fold_in(_rk, 7), (32,), 0, max(1, 256 // 4) + 1, jnp.int32)
        _lenS2 = 256 - jax.random.randint(jax.random.fold_in(_rk, 8), (32,), 0, max(1, 256 // 4) + 1, jnp.int32)
        _ctx_512P = jax.random.normal(jax.random.fold_in(_rk, 11), (32, 16, 256), jnp.float32)
        _ctx_512c = jax.random.dirichlet(jax.random.fold_in(_rk, 511), 0.3 * jnp.ones((16,), jnp.float32), (32, 256))
        _ctx_512t = jnp.einsum('bsk,bkd->bsd', _ctx_512c, _ctx_512P)
        _ctx_512t = _ctx_512t * jax.lax.rsqrt(jnp.mean(jnp.square(_ctx_512t)) + 1e-12) * 0.953939
        ctx_512 = 4.13588e-05 + 0.999923 * (_ctx_512t + 0.3 * jax.random.normal(jax.random.fold_in(_rk, 611), (32, 256, 256), jnp.float32))
        fside_BxSxS_0 = 0.000376506 + 0.999991 * jax.random.normal(jax.random.fold_in(_rk, 12), (32, 256, 256), jnp.float32)
        return (x, ctx_512, fside_BxSxS_0)
    x, ctx_512, fside_BxSxS_0 = _rec_inputs()

    def _L0_xattn_setup():
        import jax, jax.numpy as jnp
        import numpy as np
        EPS = 1e-05

        def _ln(x, g, b):
            mu = jnp.mean(x, axis=-1, keepdims=True)
            var = jnp.var(x, axis=-1, keepdims=True)
            return (x - mu) * jax.lax.rsqrt(var + EPS) * g + b

        def _cma(x1, x2, ln1_g, ln1_b, ln2_g, ln2_b, Wq, bq, Wk, bk, Wv, bv, Wo, bo):
            e = Wq.shape[1]
            scale = e ** (-0.5)
            x1n = _ln(x1, ln1_g, ln1_b)
            x2n = _ln(x2, ln2_g, ln2_b)
            q = x1n @ Wq + bq
            k = x2n @ Wk + bk
            v = x2n @ Wv + bv
            attn = jax.nn.softmax(jnp.einsum('bqe,bke->bqk', q, k) * scale, axis=-1)
            ctx = jnp.einsum('bqk,bke->bqe', attn, v)
            return ctx @ Wo + bo
        key = jax.random.key(seed)
        ks = jax.random.split(key, 24)
        B, Lt, La, Lv = (16, 256, 512, 256)
        Dt, Da, Dv, E = (512, 256, 256, 512)
        s = lambda k, *sh: jax.random.normal(k, sh, dtype=jnp.float32) * 0.02
        inp = {'text': jax.random.normal(ks[0], (B, Lt, Dt), dtype=jnp.float32), 'audio': jax.random.normal(ks[1], (B, La, Da), dtype=jnp.float32), 'video': jax.random.normal(ks[2], (B, Lv, Dv), dtype=jnp.float32), 'a_ln1_g': jnp.ones((Dt,)), 'a_ln1_b': jnp.zeros((Dt,)), 'a_ln2_g': jnp.ones((Da,)), 'a_ln2_b': jnp.zeros((Da,)), 'a_Wq': s(ks[3], Dt, E), 'a_bq': jnp.zeros((E,)), 'a_Wk': s(ks[4], Da, E), 'a_bk': jnp.zeros((E,)), 'a_Wv': s(ks[5], Da, E), 'a_bv': jnp.zeros((E,)), 'a_Wo': s(ks[6], E, Dt), 'a_bo': jnp.zeros((Dt,)), 'v_ln1_g': jnp.ones((Dt,)), 'v_ln1_b': jnp.zeros((Dt,)), 'v_ln2_g': jnp.ones((Dv,)), 'v_ln2_b': jnp.zeros((Dv,)), 'v_Wq': s(ks[7], Dt, E), 'v_bq': jnp.zeros((E,)), 'v_Wk': s(ks[8], Dv, E), 'v_bk': jnp.zeros((E,)), 'v_Wv': s(ks[9], Dv, E), 'v_bv': jnp.zeros((E,)), 'v_Wo': s(ks[10], E, Dt), 'v_bo': jnp.zeros((Dt,)), 'ln_g': jnp.ones((Dt,)), 'ln_b': jnp.zeros((Dt,)), 'fc_W': s(ks[11], Dt, Dt), 'fc_b': jnp.zeros((Dt,))}
        return inp
    _L0_xattn_all = _L0_xattn_setup()
    _L0_xattn_in = {k: v for k, v in _L0_xattn_all.items() if k in ('a_ln1_g', 'a_ln1_b', 'a_ln2_g', 'a_ln2_b', 'a_Wq', 'a_bq', 'a_Wk', 'a_bk', 'a_Wv', 'a_bv', 'a_Wo', 'a_bo', 'v_ln1_g', 'v_ln1_b', 'v_ln2_g', 'v_ln2_b', 'v_Wq', 'v_bq', 'v_Wk', 'v_bk', 'v_Wv', 'v_bv', 'v_Wo', 'v_bo', 'ln_g', 'ln_b', 'fc_W', 'fc_b')}
    del _L0_xattn_all

    def _L1_xattn_setup():
        import jax, jax.numpy as jnp
        import numpy as np
        QUERY_DIM = 512
        KEY_DIM = 256
        HIDDEN_DIM = 512
        B, LQ, LK = (8, 1024, 1024)
        key = jax.random.key(seed)
        ks = jax.random.split(key, 10)
        s_q = 1.0 / np.sqrt(QUERY_DIM)
        s_k = 1.0 / np.sqrt(KEY_DIM)
        s_h = 1.0 / np.sqrt(HIDDEN_DIM)
        return {'query': jax.random.normal(ks[0], (B, LQ, QUERY_DIM), jnp.float32), 'key': jax.random.normal(ks[1], (B, LK, KEY_DIM), jnp.float32), 'Wq': jax.random.uniform(ks[2], (QUERY_DIM, HIDDEN_DIM), jnp.float32, -s_q, s_q), 'bq': jax.random.uniform(ks[3], (HIDDEN_DIM,), jnp.float32, -s_q, s_q), 'Wk': jax.random.uniform(ks[4], (KEY_DIM, HIDDEN_DIM), jnp.float32, -s_k, s_k), 'bk': jax.random.uniform(ks[5], (HIDDEN_DIM,), jnp.float32, -s_k, s_k), 'Wv': jax.random.uniform(ks[6], (KEY_DIM, HIDDEN_DIM), jnp.float32, -s_k, s_k), 'bv': jax.random.uniform(ks[7], (HIDDEN_DIM,), jnp.float32, -s_k, s_k), 'Wo': jax.random.uniform(ks[8], (HIDDEN_DIM, QUERY_DIM), jnp.float32, -s_h, s_h), 'bo': jax.random.uniform(ks[9], (QUERY_DIM,), jnp.float32, -s_h, s_h)}
    _L1_xattn_all = _L1_xattn_setup()
    _L1_xattn_in = {k: v for k, v in _L1_xattn_all.items() if k in ('Wq', 'bq', 'Wk', 'bk', 'Wv', 'bv', 'Wo', 'bo')}
    del _L1_xattn_all
    return {'x': x, 'ctx_512': ctx_512, 'fside_BxSxS_0': fside_BxSxS_0, 'L0_xattn_a_ln1_g': _L0_xattn_in['a_ln1_g'], 'L0_xattn_a_ln1_b': _L0_xattn_in['a_ln1_b'], 'L0_xattn_a_ln2_g': _L0_xattn_in['a_ln2_g'], 'L0_xattn_a_ln2_b': _L0_xattn_in['a_ln2_b'], 'L0_xattn_a_Wq': _L0_xattn_in['a_Wq'], 'L0_xattn_a_bq': _L0_xattn_in['a_bq'], 'L0_xattn_a_Wk': _L0_xattn_in['a_Wk'], 'L0_xattn_a_bk': _L0_xattn_in['a_bk'], 'L0_xattn_a_Wv': _L0_xattn_in['a_Wv'], 'L0_xattn_a_bv': _L0_xattn_in['a_bv'], 'L0_xattn_a_Wo': _L0_xattn_in['a_Wo'], 'L0_xattn_a_bo': _L0_xattn_in['a_bo'], 'L0_xattn_v_ln1_g': _L0_xattn_in['v_ln1_g'], 'L0_xattn_v_ln1_b': _L0_xattn_in['v_ln1_b'], 'L0_xattn_v_ln2_g': _L0_xattn_in['v_ln2_g'], 'L0_xattn_v_ln2_b': _L0_xattn_in['v_ln2_b'], 'L0_xattn_v_Wq': _L0_xattn_in['v_Wq'], 'L0_xattn_v_bq': _L0_xattn_in['v_bq'], 'L0_xattn_v_Wk': _L0_xattn_in['v_Wk'], 'L0_xattn_v_bk': _L0_xattn_in['v_bk'], 'L0_xattn_v_Wv': _L0_xattn_in['v_Wv'], 'L0_xattn_v_bv': _L0_xattn_in['v_bv'], 'L0_xattn_v_Wo': _L0_xattn_in['v_Wo'], 'L0_xattn_v_bo': _L0_xattn_in['v_bo'], 'L0_xattn_ln_g': _L0_xattn_in['ln_g'], 'L0_xattn_ln_b': _L0_xattn_in['ln_b'], 'L0_xattn_fc_W': _L0_xattn_in['fc_W'], 'L0_xattn_fc_b': _L0_xattn_in['fc_b'], 'L1_xattn_Wq': _L1_xattn_in['Wq'], 'L1_xattn_bq': _L1_xattn_in['bq'], 'L1_xattn_Wk': _L1_xattn_in['Wk'], 'L1_xattn_bk': _L1_xattn_in['bk'], 'L1_xattn_Wv': _L1_xattn_in['Wv'], 'L1_xattn_bv': _L1_xattn_in['bv'], 'L1_xattn_Wo': _L1_xattn_in['Wo'], 'L1_xattn_bo': _L1_xattn_in['bo']}

def reference(x, ctx_512, fside_BxSxS_0, L0_xattn_a_ln1_g, L0_xattn_a_ln1_b, L0_xattn_a_ln2_g, L0_xattn_a_ln2_b, L0_xattn_a_Wq, L0_xattn_a_bq, L0_xattn_a_Wk, L0_xattn_a_bk, L0_xattn_a_Wv, L0_xattn_a_bv, L0_xattn_a_Wo, L0_xattn_a_bo, L0_xattn_v_ln1_g, L0_xattn_v_ln1_b, L0_xattn_v_ln2_g, L0_xattn_v_ln2_b, L0_xattn_v_Wq, L0_xattn_v_bq, L0_xattn_v_Wk, L0_xattn_v_bk, L0_xattn_v_Wv, L0_xattn_v_bv, L0_xattn_v_Wo, L0_xattn_v_bo, L0_xattn_ln_g, L0_xattn_ln_b, L0_xattn_fc_W, L0_xattn_fc_b, L1_xattn_Wq, L1_xattn_bq, L1_xattn_Wk, L1_xattn_bk, L1_xattn_Wv, L1_xattn_bv, L1_xattn_Wo, L1_xattn_bo):
    import jax
    import jax.numpy as jnp

    def _L0_xattn_ref(text, audio, video, a_ln1_g, a_ln1_b, a_ln2_g, a_ln2_b, a_Wq, a_bq, a_Wk, a_bk, a_Wv, a_bv, a_Wo, a_bo, v_ln1_g, v_ln1_b, v_ln2_g, v_ln2_b, v_Wq, v_bq, v_Wk, v_bk, v_Wv, v_bv, v_Wo, v_bo, ln_g, ln_b, fc_W, fc_b):
        import jax, jax.numpy as jnp
        import numpy as np
        EPS = 1e-05

        def _ln(x, g, b):
            mu = jnp.mean(x, axis=-1, keepdims=True)
            var = jnp.var(x, axis=-1, keepdims=True)
            return (x - mu) * jax.lax.rsqrt(var + EPS) * g + b

        def _cma(x1, x2, ln1_g, ln1_b, ln2_g, ln2_b, Wq, bq, Wk, bk, Wv, bv, Wo, bo):
            e = Wq.shape[1]
            scale = e ** (-0.5)
            x1n = _ln(x1, ln1_g, ln1_b)
            x2n = _ln(x2, ln2_g, ln2_b)
            q = x1n @ Wq + bq
            k = x2n @ Wk + bk
            v = x2n @ Wv + bv
            attn = jax.nn.softmax(jnp.einsum('bqe,bke->bqk', q, k) * scale, axis=-1)
            ctx = jnp.einsum('bqk,bke->bqe', attn, v)
            return ctx @ Wo + bo
        out_a = _cma(text, audio, a_ln1_g, a_ln1_b, a_ln2_g, a_ln2_b, a_Wq, a_bq, a_Wk, a_bk, a_Wv, a_bv, a_Wo, a_bo)
        out_v = _cma(text, video, v_ln1_g, v_ln1_b, v_ln2_g, v_ln2_b, v_Wq, v_bq, v_Wk, v_bk, v_Wv, v_bv, v_Wo, v_bo)
        output = out_a + out_v + text
        residual = output
        output = _ln(output, ln_g, ln_b) @ fc_W + fc_b
        return output + residual

    def _L1_xattn_ref(query, key, Wq, bq, Wk, bk, Wv, bv, Wo, bo):
        import jax, jax.numpy as jnp
        import numpy as np
        QUERY_DIM = 512
        KEY_DIM = 256
        HIDDEN_DIM = 512
        B, LQ, LK = (8, 1024, 1024)
        scale = HIDDEN_DIM ** (-0.5)
        Q = jnp.einsum('bqd,dh->bqh', query, Wq) + bq
        K = jnp.einsum('bkd,dh->bkh', key, Wk) + bk
        V = jnp.einsum('bkd,dh->bkh', key, Wv) + bv
        scores = jnp.einsum('bqh,bkh->bqk', Q, K) * scale
        weights = jax.nn.softmax(scores, axis=-1)
        attended = jnp.einsum('bqk,bkh->bqh', weights, V)
        out = jnp.einsum('bqh,hd->bqd', attended, Wo) + bo
        return query + out
    x = _L0_xattn_ref(x, ctx_512, fside_BxSxS_0, L0_xattn_a_ln1_g, L0_xattn_a_ln1_b, L0_xattn_a_ln2_g, L0_xattn_a_ln2_b, L0_xattn_a_Wq, L0_xattn_a_bq, L0_xattn_a_Wk, L0_xattn_a_bk, L0_xattn_a_Wv, L0_xattn_a_bv, L0_xattn_a_Wo, L0_xattn_a_bo, L0_xattn_v_ln1_g, L0_xattn_v_ln1_b, L0_xattn_v_ln2_g, L0_xattn_v_ln2_b, L0_xattn_v_Wq, L0_xattn_v_bq, L0_xattn_v_Wk, L0_xattn_v_bk, L0_xattn_v_Wv, L0_xattn_v_bv, L0_xattn_v_Wo, L0_xattn_v_bo, L0_xattn_ln_g, L0_xattn_ln_b, L0_xattn_fc_W, L0_xattn_fc_b)
    x = _L1_xattn_ref(x, ctx_512, L1_xattn_Wq, L1_xattn_bq, L1_xattn_Wk, L1_xattn_bk, L1_xattn_Wv, L1_xattn_bv, L1_xattn_Wo, L1_xattn_bo)
    return x

_drawn_inputs = setup_inputs


def setup_inputs(seed=0):
    import zlib

    import numpy as np

    out = dict(_drawn_inputs(seed))
    spreads = {'L0_xattn_a_ln1_g': (1.0, 0.6),
     'L0_xattn_a_ln1_b': (0.0, 0.8),
     'L0_xattn_a_ln2_g': (1.0, 0.6),
     'L0_xattn_a_ln2_b': (0.0, 0.571),
     'L0_xattn_a_bq': (0.0, 0.8),
     'L0_xattn_a_bk': (0.0, 2.0),
     'L0_xattn_a_bv': (0.0, 0.1),
     'L0_xattn_a_bo': (0.0, 0.1),
     'L0_xattn_v_ln1_g': (1.0, 0.6),
     'L0_xattn_v_ln1_b': (0.0, 0.8),
     'L0_xattn_v_ln2_g': (1.0, 0.6),
     'L0_xattn_v_ln2_b': (0.0, 0.591),
     'L0_xattn_v_bq': (0.0, 0.8),
     'L0_xattn_v_bk': (0.0, 2.0),
     'L0_xattn_v_bv': (0.0, 0.1),
     'L0_xattn_v_bo': (0.0, 0.1),
     'L0_xattn_ln_g': (1.0, 0.2),
     'L0_xattn_ln_b': (0.0, 0.1),
     'L0_xattn_fc_b': (0.0, 0.1)}
    factors = {'fside_BxSxS_0': 6.114,
     'L0_xattn_a_Wq': 8.0,
     'L0_xattn_a_Wk': 8.0,
     'L0_xattn_v_Wq': 8.0,
     'L0_xattn_v_Wk': 8.0,
     'L0_xattn_v_Wv': 3.522,
     'L1_xattn_Wq': 2.766,
     'L1_xattn_bq': 8.0,
     'L1_xattn_Wk': 2.755,
     'L1_xattn_bk': 64.0,
     'L1_xattn_bv': 3.238,
     'L1_xattn_bo': 3.118}
    for name, (base, spread) in spreads.items():
        noise = np.random.default_rng([zlib.crc32(name.encode()), seed]).standard_normal(out[name].shape)
        drawn = base * np.exp(spread * noise) if base else spread * noise
        out[name] = jnp.asarray(drawn.astype(out[name].dtype))
    for name, factor in factors.items():
        out[name] = (out[name] * factor).astype(out[name].dtype)
    return out
```

```python
from contextlib import ExitStack

import concourse.bass as bass
from concourse import mybir

F32 = mybir.dt.float32
F32R = mybir.dt.float32r
ALU = mybir.AluOpType
ACT = mybir.ActivationFunctionType
AX = mybir.AxisListType

P = 128
EPS = 1e-5
HI, LO = 0, 1

VECTORS = [(f"{k}_{name}", width) for k in ("a", "v")
           for name, width in (("g1", 512), ("b1", 512), ("g2", 256), ("b2", 256), ("bq", 512), ("bk", 512), ("bv", 512))]
VECTORS += [("1_bq", 512), ("1_bk", 512), ("1_bv", 512), ("ln_g", 512), ("ln_b", 512)]
ROWS = [("a_g2", 256), ("v_g2", 256), ("a_bo", 512), ("v_bo", 512), ("fc_b", 512), ("1_bo", 512)]


def build_kernel(nc, x, ctx, ctxT, fside, vectors, rows, weights, fc_W, out):
    B, L, D = x.shape
    K, C = ctx.shape[1:]
    E = weights["a"]["Wo"].shape[0]
    NT, NK, ND, NC, NE = L // P, K // P, D // P, C // P, E // P
    SCALE = float(E) ** -0.5
    ATT = ("a", "v", "1")
    assert NT * C == 512 and NC * L == 512 and NK * L == 512 and D == 512 and E == 512

    vector_at, at = {}, 0
    for name, width in VECTORS:
        vector_at[name] = (at, width // P)
        at += width // P
    n_columns = at

    with ExitStack() as whole:
        def sb(name, shape, dt=F32):
            return whole.enter_context(nc.sbuf_tensor("s_" + name, shape, dt))

        M = {k: sb(f"M_{k}", [P, 2, ND, C], F32R) for k in ATT}
        Wvo = {k: sb(f"Wvo_{k}", [P, 2, NC, D], F32R) for k in ATT}
        Wfc = sb("Wfc", [P, 2, ND, D], F32R)
        m = {k: sb(f"m_{k}", [P, NC]) for k in ATT}
        u = {k: sb(f"u_{k}", [P, D]) for k in ATT}
        u0 = {k: sb(f"u0_{k}", [P, 1]) for k in ATT}
        bias_attn = sb("bias_attn", [P, D])
        bias_fc = sb("bias_fc", [P, D])
        bias_1 = sb("bias_1", [P, D])
        ident = sb("ident", [P, P])
        banks = [whole.enter_context(nc.psum_tensor(f"bank{j}", [P, 512], F32)) for j in range(8)]

        setup_phase(nc, vector_at, n_columns, SCALE, vectors, rows, weights, fc_W,
                    M, Wvo, Wfc, m, u, u0, bias_attn, bias_fc, bias_1, ident, banks,
                    (ND, NC, NE, D, C))
        main_phase(nc, SCALE, x, ctx, ctxT, fside, out, M, Wvo, Wfc, m, u, u0,
                   bias_attn, bias_fc, bias_1, ident, banks, (B, L, D, K, C, NT, NK, ND, NC))


def setup_phase(nc, vector_at, n_columns, SCALE, vectors, rows, weights, fc_W,
                M, Wvo, Wfc, m, u, u0, bias_attn, bias_fc, bias_1, ident, banks, sizes):
    ND, NC, NE, D, C = sizes
    ATT = ("a", "v", "1")
    with ExitStack() as ctx:
        def sb(name, shape, dt=F32):
            return ctx.enter_context(nc.sbuf_tensor("w_" + name, shape, dt))

        def sem(name):
            return ctx.enter_context(nc.semaphore("w_" + name))

        cols = sb("cols", [P, n_columns])
        row = {name: sb(f"row_{name}", [P, width]) for name, width in ROWS}
        raw = [dict(WqT=sb(f"WqT{j}", [P, NE, D]), WkT=sb(f"WkT{j}", [P, NE, C]),
                               Wk=sb(f"Wk{j}", [P, NC, NE * P]), WvT=sb(f"WvT{j}", [P, NE, C]),
                               Wv=sb(f"Wv{j}", [P, NC, NE * P]), Wo=sb(f"Wo{j}", [P, NE, D])) for j in range(2)]
        G = sb("G", [P, ND, C])
        scaled = sb("scaled", [P, 4, 256])
        kb = {k: sb(f"kb_{k}", [P, NE]) for k in ("a", "v")}
        vb = {k: sb(f"vb_{k}", [P, NE]) for k in ("a", "v")}
        qk = sb("qk", [P, ND])
        ucol = sb("ucol", [P, ND])
        raw_fc = sb("raw_fc", [P, ND, D])

        loaded = {k: sem(f"loaded_{k}") for k in ("vec", "fc") + ATT}
        ident_ready = sem("ident_ready")
        G_done, H_done, kvb_done, mq_done, u_done, row_done = (
            sem(f"{n}_done") for n in ("G", "H", "kvb", "mq", "u", "row"))
        G_copied, kvb_ready, ucol_ready, small_ready = (
            sem(n) for n in ("G_copied", "kvb_ready", "ucol_ready", "small_ready"))
        M_scaled, M_high, M_split = (sem(n) for n in ("M_scaled", "M_high", "M_split"))
        O_scaled, O_high, O_split = (sem(n) for n in ("O_scaled", "O_high", "O_split"))
        u_copied, row_copied, fc_row_done, fc_step = (
            sem(n) for n in ("u_copied", "row_copied", "fc_row_done", "fc_step"))

        def column(name, j=None):
            at, width = vector_at[name]
            return cols[:, at:at + width] if j is None else cols[:, at + j:at + j + 1]

        def kbias(k):
            return kb[k] if k in kb else column(k + "_bk")

        def vbias(k):
            return vb[k] if k in vb else column(k + "_bv")

        G_bank, H_bank = banks[0:2], banks[2:4]
        small_bank, u_bank, row_bank = banks[4], banks[5], banks[6]
        kb_at, vb_at, m_at, qk_at, u0_at = 0, 4, 8, 12, 16

        block = ctx.enter_context(nc.Block())

        @block.sync
        def _(sp):
            sp.dma_start(cols[:, :], vectors).then_inc(loaded["vec"], 16)
            for n, k in enumerate(ATT):
                w, r = weights[k], raw[n % 2]
                if n >= 2:
                    sp.wait_ge(row_done, n - 1)
                    sp.wait_ge(H_done, n - 1)
                    sp.wait_ge(u_done, n - 1)
                for name in ("WqT", "WkT", "WvT", "Wo") + (("Wk", "Wv") if k in kb else ()):
                    sp.dma_start(r[name][:, :, :], w[name].rearrange("(c p) n -> p c n", p=P)).then_inc(loaded[k], 16)
                if n == 0:
                    for name, _ in ROWS:
                        sp.dma_start(row[name][:, :], rows[name].partition_broadcast(P)).then_inc(loaded["vec"], 16)
            sp.dma_start(raw_fc[:, :, :], fc_W.rearrange("(c p) n -> p c n", p=P)).then_inc(loaded["fc"], 16)

        @block.gpsimd
        def _(pool):
            pool.memset(ident[:, :], 0.0).then_inc(ident_ready, 1)
            pool.wait_ge(ident_ready, 1)
            pool.affine_select(out=ident[:, :], in_=ident[:, :], compare_op=ALU.not_equal, fill=1.0, base=0,
                               pattern=[[-1, P]], channel_multiplier=1).then_inc(ident_ready, 1)

        all_vectors = 16 * (1 + len(ROWS))

        @block.tensor
        def _(pe):
            def spread(col):
                return col.to_broadcast([P, P])

            pe.wait_ge(loaded["vec"], all_vectors)
            for n, k in enumerate(ATT):
                w = raw[n % 2]
                normed = k in kb
                pe.wait_ge(loaded[k], 16 * (6 if normed else 4))
                if n:
                    pe.wait_ge(M_split, n)
                for i in range(ND):
                    for e in range(NE):
                        mm = pe.matmul(G_bank[i // 2][:, (i % 2) * C:(i % 2 + 1) * C], w["WqT"][:, e, i * P:(i + 1) * P],
                                       w["WkT"][:, e, :], start=e == 0, stop=e == NE - 1)
                mm.then_inc(G_done, 1)
                if normed:
                    if n:
                        pe.wait_ge(small_ready, n)
                    for at, mat in ((kb_at, w["Wk"]), (vb_at, w["Wv"])):
                        for e in range(NE):
                            for c in range(NC):
                                mm = pe.matmul(small_bank[:, at + e:at + e + 1], mat[:, c, e * P:(e + 1) * P],
                                               column(k + "_b2", c), start=c == 0, stop=c == NC - 1)
                    mm.then_inc(kvb_done, 1)
                if n:
                    pe.wait_ge(O_split, n)
                for j in range(NC):
                    for e in range(NE):
                        mm = pe.matmul(H_bank[j][:, :], w["WvT"][:, e, j * P:(j + 1) * P], w["Wo"][:, e, :],
                                       start=e == 0, stop=e == NE - 1)
                mm.then_inc(H_done, 1)
                if normed:
                    pe.wait_ge(kvb_ready, n + 1)
                else:
                    pe.wait_ge(small_ready, n)
                pe.wait_ge(G_copied, n + 1)
                for c in range(NC):
                    for e in range(NE):
                        pe.matmul(small_bank[:, m_at + c:m_at + c + 1], w["WkT"][:, e, c * P:(c + 1) * P],
                                  column(k + "_bq", e), start=e == 0, stop=not normed and e == NE - 1)
                    if normed:
                        for i in range(ND):
                            pe.matmul(small_bank[:, m_at + c:m_at + c + 1], G[:, i, c * P:(c + 1) * P],
                                      column(k + "_b1", i), start=False, stop=i == ND - 1)
                for i in range(ND):
                    for e in range(NE):
                        mm = pe.matmul(small_bank[:, qk_at + i:qk_at + i + 1], w["WqT"][:, e, i * P:(i + 1) * P],
                                       kbias(k)[:, e:e + 1], start=e == 0, stop=e == NE - 1)
                mm.then_inc(mq_done, 1)
                pe.wait_ge(ucol_ready, n + 1)
                for e in range(NE):
                    mm = pe.matmul(small_bank[:, u0_at:u0_at + 1], spread(column(k + "_bq", e)), kbias(k)[:, e:e + 1],
                                   start=e == 0, stop=not normed and e == NE - 1)
                if normed:
                    for i in range(ND):
                        mm = pe.matmul(small_bank[:, u0_at:u0_at + 1], spread(column(k + "_b1", i)), qk[:, i:i + 1],
                                       start=False, stop=i == ND - 1)
                pe.wait_ge(ident_ready, 2)
                if n:
                    pe.wait_ge(u_copied, n)
                for i in range(ND):
                    mm = pe.matmul(u_bank[:, i * P:(i + 1) * P], spread(ucol[:, i:i + 1]), ident[:, :],
                                   start=True, stop=True)
                mm.then_inc(u_done, 1)
                if k == "1":
                    pe.wait_ge(row_copied, 1)
                for e in range(NE):
                    mm = pe.matmul(row_bank[:, :], spread(vbias(k)[:, e:e + 1]), w["Wo"][:, e, :],
                                   start=e == 0 and k != "v", stop=e == NE - 1 and k != "a")
                mm.then_inc(row_done, 1)
            pe.wait_ge(loaded["fc"], 16)
            pe.wait_ge(row_copied, 2)
            for i in range(ND):
                mm = pe.matmul(row_bank[:, :], spread(column("ln_b", i)), raw_fc[:, i, :],
                               start=i == 0, stop=i == ND - 1)
            mm.then_inc(fc_row_done, 1)

        @block.scalar
        def _(act):
            for n, k in enumerate(ATT):
                act.wait_ge(G_done, n + 1)
                if n:
                    act.wait_ge(mq_done, n)
                for b in range(2):
                    ins = act.copy(G[:, 2 * b:2 * b + 2, :].rearrange("p a b -> p (a b)"), G_bank[b][:, :])
                ins.then_inc(G_copied, 1)
                act.wait_ge(M_scaled, n + 1)
                act.copy(M[k][:, HI, :, :], scaled[:, :, :]).then_inc(M_high, 1)
                act.wait_ge(O_scaled, n + 1)
                act.copy(Wvo[k][:, HI, :, :].rearrange("p a b -> p (a b)"),
                         scaled[:, :, :].rearrange("p a b -> p (a b)")).then_inc(O_high, 1)

        @block.vector
        def _(dve):
            dve.wait_ge(loaded["vec"], all_vectors)
            for n, k in enumerate(ATT):
                normed = k in kb
                dve.wait_ge(G_copied, n + 1)
                for i in range(ND):
                    part = G_bank[i // 2][:, (i % 2) * C:(i % 2 + 1) * C]
                    if normed:
                        ins = dve.scalar_tensor_tensor(out=scaled[:, i, :], in0=part, scalar=column(k + "_g1", i),
                                                       in1=row[k + "_g2"][:, :], op0=ALU.mult, op1=ALU.mult)
                    else:
                        ins = dve.tensor_copy(scaled[:, i, :], part)
                ins.then_inc(M_scaled, 1)
                dve.wait_ge(M_scaled, n + 1)
                dve.wait_ge(M_high, n + 1)
                dve.tensor_tensor(M[k][:, LO, :, :], scaled[:, :, :], M[k][:, HI, :, :],
                                  ALU.subtract).then_inc(M_split, 1)
                if normed:
                    dve.wait_ge(kvb_done, n + 1)
                    dve.tensor_tensor(kb[k][:, :], small_bank[:, kb_at:kb_at + NE], column(k + "_bk"), ALU.add)
                    dve.tensor_tensor(vb[k][:, :], small_bank[:, vb_at:vb_at + NE], column(k + "_bv"),
                                      ALU.add).then_inc(kvb_ready, 1)
                dve.wait_ge(H_done, n + 1)
                dve.wait_ge(M_split, n + 1)
                for c in range(NC):
                    part = scaled[:, 2 * c:2 * c + 2, :].rearrange("p a b -> p (a b)")
                    if normed:
                        ins = dve.tensor_scalar(part, H_bank[c][:, :], column(k + "_g2", c), None, ALU.mult)
                    else:
                        ins = dve.tensor_copy(part, H_bank[c][:, :])
                ins.then_inc(O_scaled, 1)
                dve.wait_ge(O_scaled, n + 1)
                dve.wait_ge(O_high, n + 1)
                dve.tensor_tensor(Wvo[k][:, LO, :, :].rearrange("p a b -> p (a b)"),
                                  scaled[:, :, :].rearrange("p a b -> p (a b)"),
                                  Wvo[k][:, HI, :, :].rearrange("p a b -> p (a b)"),
                                  ALU.subtract).then_inc(O_split, 1)
                dve.wait_ge(O_split, n + 1)
                dve.wait_ge(mq_done, n + 1)
                if n:
                    dve.wait_ge(u_done, n)
                dve.tensor_copy(qk[:, :], small_bank[:, qk_at:qk_at + ND])
                if normed:
                    dve.tensor_tensor(m[k][:, :], small_bank[:, m_at:m_at + NC], column(k + "_g2"), ALU.mult)
                    dve.tensor_tensor(ucol[:, :], small_bank[:, qk_at:qk_at + ND], column(k + "_g1"),
                                      ALU.mult).then_inc(ucol_ready, 1)
                else:
                    dve.tensor_copy(m[k][:, :], small_bank[:, m_at:m_at + NC])
                    dve.tensor_copy(ucol[:, :], small_bank[:, qk_at:qk_at + ND]).then_inc(ucol_ready, 1)
                dve.wait_ge(u_done, n + 1)
                dve.tensor_scalar(u0[k][:, :], small_bank[:, u0_at:u0_at + 1], SCALE, None,
                                  ALU.mult).then_inc(small_ready, 1)
                dve.tensor_copy(u[k][:, :], u_bank[:, :]).then_inc(u_copied, 1)
                if k == "v":
                    dve.wait_ge(row_done, 2)
                    dve.tensor_tensor(bias_attn[:, :], row_bank[:, :], row["a_bo"][:, :], ALU.add).then_inc(row_copied, 1)
                    dve.wait_ge(row_copied, 1)
                    dve.tensor_tensor(bias_attn[:, :], bias_attn[:, :], row["v_bo"][:, :], ALU.add)
                if k == "1":
                    dve.wait_ge(row_done, 3)
                    dve.tensor_tensor(bias_1[:, :], row_bank[:, :], row["1_bo"][:, :], ALU.add).then_inc(row_copied, 1)
            dve.wait_ge(loaded["fc"], 16)
            dve.wait_ge(fc_row_done, 1)
            dve.tensor_tensor(bias_fc[:, :], row_bank[:, :], row["fc_b"][:, :], ALU.add)
            for i in range(ND):
                ins = dve.tensor_scalar(raw_fc[:, i, :], raw_fc[:, i, :], column("ln_g", i), None, ALU.mult)
            ins.then_inc(fc_step, 1)
            dve.wait_ge(fc_step, 1)
            dve.tensor_copy(Wfc[:, HI, :, :], raw_fc[:, :, :]).then_inc(fc_step, 1)
            dve.wait_ge(fc_step, 2)
            dve.tensor_tensor(Wfc[:, LO, :, :], raw_fc[:, :, :], Wfc[:, HI, :, :], ALU.subtract)


def main_phase(nc, SCALE, x, ctx, ctxT, fside, out, M, Wvo, Wfc, m, u, u0,
               bias_attn, bias_fc, bias_1, ident, banks, sizes):
    B, L, D, K, C, NT, NK, ND, NC = sizes
    with ExitStack() as stack:
        def sb(name, shape, dt=F32):
            return stack.enter_context(nc.sbuf_tensor("t_" + name, shape, dt))

        def sem(name):
            return stack.enter_context(nc.semaphore(name))

        x_in, x_hat, x_bias, o, o_hat, y = (sb(n, [P, NT, D]) for n in ("x_in", "x_hat", "x_bias", "o", "o_hat", "y"))
        ctx_in, fside_in, ctx1_in, a_hat, v_hat = (
            sb(n, [P, NK, C]) for n in ("ctx_in", "fside_in", "ctx1_in", "a_hat", "v_hat"))
        ctxT1_in = sb("ctxT1_in", [P, NC, K])
        xT, oT, yT = (sb(n, [P, 2, ND, L], F32R) for n in ("xT", "oT", "yT"))
        kT, rows, qT, pT, cT = ({k: sb(f"{n}_{k}", [P, 2, 2, 256], F32R) for k in "av1"}
                                for n in ("kT", "rows", "qT", "pT", "cT"))
        probs = {k: sb(f"probs_{k}", [P, NT, K]) for k in "av1"}
        product = sb("product", [P, NT, D])
        shift = {k: sb(f"shift_{k}", [P, NT]) for k in "av1"}
        top = {k: sb(f"top_{k}", [P, NT]) for k in "av1"}
        total = {k: sb(f"total_{k}", [P, NT]) for k in "av1"}
        exp_bias = {k: sb(f"exp_bias_{k}", [P, NT]) for k in "av1"}
        row_sum = {k: sb(f"row_sum_{k}", [P, NT]) for k in "av1"}
        inverse = {k: sb(f"inverse_{k}", [P, NT]) for k in "av1"}
        NS = 3 * 2
        stats, moments = sb("stats", [P, NS, 6]), sb("moments", [P, NS, 2])
        var, rstd, neg_mean, offset = (sb(n, [P, NS]) for n in ("var", "rstd", "neg_mean", "offset"))
        o_stats, o_moments = sb("o_stats", [P, NT, 6]), sb("o_moments", [P, NT, 2])
        o_var, o_rstd, o_neg_mean, o_offset = (sb(n, [P, NT]) for n in ("o_var", "o_rstd", "o_neg_mean", "o_offset"))
        power = sb("power", [P, NS])

        A0, A1, A2, F0, F1, F2, N0, N1 = banks

        names = """
            x_loaded ctx_loaded fside_loaded ctx1_loaded ctxT1_loaded out0_stored out1_stored
            q_a_done q_v_done q_1_done s_a_done s_v_done s_1_done pT_a_done pT_v_done pT_1_done
            c_a_done c_v_done c_1_done xT0_done xT1_done oT0_done oT1_done yT0_done yT1_done
            kT_a_done kT_v_done attn0_done attn1_done fc0_done fc1_done z0_done z1_done
            q_a_high q_v_high q_1_high pT_a_high pT_v_high pT_1_high c_a_high c_v_high c_1_high
            xT0_high xT1_high oT0_high oT1_high yT0_high yT1_high kT_a_high kT_v_high kT_1_high
            rows_a_high rows_v_high rows_1_high
            q_a_split q_v_split q_1_split pT_a_split pT_v_split pT_1_split c_a_split c_v_split c_1_split
            xT0_split xT1_split oT0_split oT1_split yT0_split yT1_split kT_a_split kT_v_split kT_1_split
            rows_a_split rows_v_split rows_1_split
            top_a top_v top_1 total_a total_v total_1 bias_a bias_v bias_1 exp_a exp_v exp_1
            inverse_a inverse_v inverse_1 probs_a probs_v probs_1 shift_a shift_v shift_1
            stats_ready moments_ready var_ready rstd_ready o_stats_ready o_moments_ready o_var_ready
            o_rstd_ready offset_ready o_offset_ready x_hat_ready a_hat_ready v_hat_ready o_hat_ready x_bias_ready o_bias_ready
            y_bias_ready o0_ready o1_ready y0_ready y1_ready z0_ready z1_ready power_set
        """.split()
        s = {n: sem(n) for n in names}

        x_rows = x.rearrange("b (t p) d -> b p t d", p=P)
        ctx_rows = ctx.rearrange("b (t p) d -> b p t d", p=P)
        ctxT_rows = ctxT.rearrange("b (t p) d -> b p t d", p=P)
        fside_rows = fside.rearrange("b (t p) d -> b p t d", p=P)
        out_rows = out.rearrange("b (t p) d -> b p t d", p=P)

        block = stack.enter_context(nc.Block())

        HEAD = [(-1, "N"), (0, "NA"), (1, "NAF")]
        TAIL = [(B - 1, "AFZ"), (B, "FZ"), (B + 1, "Z")]

        def all_iterations(engine, iteration):
            for i, stages in HEAD:
                iteration(i, stages)
            with engine.Fori(2, B - 1) as i:
                iteration(i, "NAFZ")
            for i, stages in TAIL:
                iteration(i, stages)

        @block.sync
        def _(sp):
            def iteration(i, stages):
                n, a, f, z = i + 1, i, i - 1, i - 2
                if "F" in stages:
                    sp.wait_ge(s["rows_1_split"], f)
                    sp.dma_start(ctx1_in[:, :, :], ctx_rows[f]).then_inc(s["ctx1_loaded"], 16)
                    sp.wait_ge(s["kT_1_split"], f)
                    sp.dma_start(ctxT1_in[:, :, :], ctxT_rows[f]).then_inc(s["ctxT1_loaded"], 16)
                if "N" in stages:
                    sp.wait_ge(s["a_hat_ready"], n)
                    sp.dma_start(ctx_in[:, :, :], ctx_rows[n]).then_inc(s["ctx_loaded"], 16)
                    sp.wait_ge(s["v_hat_ready"], n)
                    sp.dma_start(fside_in[:, :, :], fside_rows[n]).then_inc(s["fside_loaded"], 16)
                    sp.wait_ge(s["x_bias_ready"], n)
                    sp.dma_start(x_in[:, :, :], x_rows[n]).then_inc(s["x_loaded"], 16)
                if "Z" in stages:
                    sp.wait_ge(s["z0_ready"], z + 1)
                    sp.dma_start(out_rows[z, :, 0], y[:, 0, :]).then_inc(s["out0_stored"], 16)
                    sp.wait_ge(s["z1_ready"], z + 1)
                    sp.dma_start(out_rows[z, :, 1], y[:, 1, :]).then_inc(s["out1_stored"], 16)

            all_iterations(sp, iteration)
            sp.wait_ge(s["out0_stored"], 16 * B)
            sp.wait_ge(s["out1_stored"], 16 * B)

        @block.tensor
        def _(pe):
            def product3(out, left, right, chunks):
                passes = [(h, g) for h, g in ((HI, HI), (HI, LO), (LO, HI))]
                for c in range(chunks):
                    for h, g in passes:
                        mm = pe.matmul(out, left(h, c), right(g, c), start=c == 0 and (h, g) == (HI, HI),
                                       stop=c == chunks - 1 and (h, g) == (LO, HI))
                return mm

            def project(bank, k, source):
                for j in range(NC):
                    mm = product3(bank[:, j * L:(j + 1) * L], lambda h, c: M[k][:, h, c, j * P:(j + 1) * P],
                                  lambda g, c: source[:, g, c, :], ND)
                return mm

            def scores(bank, k):
                for t in range(NT):
                    mm = product3(bank[:, t * K:(t + 1) * K], lambda h, c: qT[k][:, h, c, t * P:(t + 1) * P],
                                  lambda g, c: kT[k][:, g, c, :], NC)
                return mm

            def turn(bank, blocks):
                for j, b in enumerate(blocks):
                    mm = pe.transpose(bank[:, j * P:(j + 1) * P], b, ident[:, :])
                return mm

            def turned_probs(k):
                return [probs[k][:, t, c * P:(c + 1) * P] for c in range(NK) for t in range(NT)]

            def mix(bank, k):
                for j in range(NC):
                    mm = product3(bank[:, j * L:(j + 1) * L], lambda h, c: rows[k][:, h, c, j * P:(j + 1) * P],
                                  lambda g, c: pT[k][:, g, c, :], NK)
                return mm

            def turned(tile, half):
                return [tile[:, t, c * P:(c + 1) * P] for c in (2 * half, 2 * half + 1) for t in range(NT)]

            def attention_out(bank, t):
                for k in "av":
                    for c in range(NC):
                        for h, g in ((HI, HI), (HI, LO), (LO, HI)):
                            mm = pe.matmul(bank[:, :], cT[k][:, h, c, t * P:(t + 1) * P], Wvo[k][:, g, c, :],
                                           start=k == "a" and c == 0 and (h, g) == (HI, HI),
                                           stop=k == "v" and c == NC - 1 and (h, g) == (LO, HI))
                return mm

            def iteration(i, stages):
                n, a, f, z = i + 1, i, i - 1, i - 2
                if "A" in stages:
                    pe.wait_ge(s["xT0_split"], a + 1)
                    pe.wait_ge(s["xT1_split"], a + 1)
                    project(A0, "a", xT).then_inc(s["q_a_done"], 1)
                if "Z" in stages:
                    pe.wait_ge(s["rows_1_split"], z + 1)
                    pe.wait_ge(s["pT_1_split"], z + 1)
                    mix(F0, "1").then_inc(s["c_1_done"], 1)
                if "A" in stages:
                    pe.wait_ge(s["o1_ready"], a)
                    project(A1, "v", xT).then_inc(s["q_v_done"], 1)
                if "F" in stages:
                    pe.wait_ge(s["o_hat_ready"], f + 1)
                    pe.wait_ge(s["exp_1"], f)
                    turn(F1, turned(o_hat, 0)).then_inc(s["oT0_done"], 1)
                    pe.wait_ge(s["pT_1_split"], f)
                    turn(F2, turned(o_hat, 1)).then_inc(s["oT1_done"], 1)
                if "Z" in stages:
                    pe.wait_ge(s["c_1_split"], z + 1)
                    if "A" in stages:
                        pe.wait_ge(s["kT_a_split"], a + 1)
                        pe.wait_ge(s["kT_v_split"], a + 1)
                    product3(N0[:, :], lambda h, c: cT["1"][:, h, c, 0:P],
                             lambda g, c: Wvo["1"][:, g, c, :], NC).then_inc(s["z0_done"], 1)
                    product3(N1[:, :], lambda h, c: cT["1"][:, h, c, P:2 * P],
                             lambda g, c: Wvo["1"][:, g, c, :], NC).then_inc(s["z1_done"], 1)
                if "A" in stages:
                    pe.wait_ge(s["q_a_split"], a + 1)
                    pe.wait_ge(s["kT_a_split"], a + 1)
                    pe.wait_ge(s["o0_ready"], a)
                    scores(A2, "a").then_inc(s["s_a_done"], 1)
                    pe.wait_ge(s["q_v_split"], a + 1)
                    pe.wait_ge(s["kT_v_split"], a + 1)
                    scores(A0, "v").then_inc(s["s_v_done"], 1)
                if "F" in stages:
                    pe.wait_ge(s["oT0_split"], f + 1)
                    pe.wait_ge(s["oT1_split"], f + 1)
                    product3(F2[:, :], lambda h, c: oT[:, h, c, 0:P],
                             lambda g, c: Wfc[:, g, c, :], ND).then_inc(s["fc0_done"], 1)
                    product3(F0[:, :], lambda h, c: oT[:, h, c, P:2 * P],
                             lambda g, c: Wfc[:, g, c, :], ND).then_inc(s["fc1_done"], 1)
                if "A" in stages:
                    pe.wait_ge(s["probs_a"], a + 1)
                    turn(A1, turned_probs("a")).then_inc(s["pT_a_done"], 1)
                    pe.wait_ge(s["probs_v"], a + 1)
                    turn(A2, turned_probs("v")).then_inc(s["pT_v_done"], 1)
                if "N" in stages:
                    pe.wait_ge(s["x_hat_ready"], n + 1)
                    if "Z" in stages:
                        pe.wait_ge(s["z0_ready"], z + 1)
                        pe.wait_ge(s["z1_ready"], z + 1)
                    turn(N0, turned(x_hat, 0)).then_inc(s["xT0_done"], 1)
                    turn(N1, turned(x_hat, 1)).then_inc(s["xT1_done"], 1)
                if "F" in stages:
                    pe.wait_ge(s["y1_ready"], f + 1)
                    turn(F1, turned(y, 0)).then_inc(s["yT0_done"], 1)
                    turn(F2, turned(y, 1)).then_inc(s["yT1_done"], 1)
                if "A" in stages:
                    pe.wait_ge(s["rows_a_split"], a + 1)
                    pe.wait_ge(s["pT_a_split"], a + 1)
                    mix(A0, "a").then_inc(s["c_a_done"], 1)
                    pe.wait_ge(s["rows_v_split"], a + 1)
                    pe.wait_ge(s["pT_v_split"], a + 1)
                    mix(A1, "v").then_inc(s["c_v_done"], 1)
                if "F" in stages:
                    pe.wait_ge(s["yT0_split"], f + 1)
                    pe.wait_ge(s["yT1_split"], f + 1)
                    project(F0, "1", yT).then_inc(s["q_1_done"], 1)
                if "A" in stages:
                    pe.wait_ge(s["c_a_split"], a + 1)
                    pe.wait_ge(s["c_v_split"], a + 1)
                    attention_out(A2, 0).then_inc(s["attn0_done"], 1)
                if "F" in stages:
                    pe.wait_ge(s["q_1_split"], f + 1)
                    pe.wait_ge(s["kT_1_split"], f + 1)
                    scores(F1, "1").then_inc(s["s_1_done"], 1)
                if "A" in stages:
                    attention_out(A1, 1).then_inc(s["attn1_done"], 1)
                if "N" in stages:
                    pe.wait_ge(s["a_hat_ready"], n + 1)
                    pe.wait_ge(s["xT0_split"], n + 1)
                    turn(N0, [a_hat[:, t, c * P:(c + 1) * P] for c in range(NC) for t in range(NK)]).then_inc(s["kT_a_done"], 1)
                    pe.wait_ge(s["v_hat_ready"], n + 1)
                    pe.wait_ge(s["xT1_split"], n + 1)
                    turn(N1, [v_hat[:, t, c * P:(c + 1) * P] for c in range(NC) for t in range(NK)]).then_inc(s["kT_v_done"], 1)
                if "F" in stages:
                    pe.wait_ge(s["probs_1"], f + 1)
                    turn(F2, turned_probs("1")).then_inc(s["pT_1_done"], 1)

            all_iterations(pe, iteration)

        def halves(tile, part, half):
            return tile[:, part, 2 * half:2 * half + 2, :].rearrange("p c l -> p (c l)")

        def flat(tile, part):
            return tile[:, part, :, :].rearrange("p c l -> p (c l)")

        @block.scalar
        def _(act):
            def high(target, bank, name, count):
                act.wait_ge(s[name + "_done"], count)
                act.copy(target, bank[:, :]).then_inc(s[name + "_high"], 1)

            def high_q(k, bank, count):
                act.wait_ge(s[f"q_{k}_done"], count)
                act.activation(qT[k][:, HI, 0, :], bank[:, 0:L], ACT.Identity, bias=m[k][:, 0:1])
                act.activation(qT[k][:, HI, 1, :], bank[:, L:2 * L], ACT.Identity,
                               bias=m[k][:, 1:2]).then_inc(s[f"q_{k}_high"], 1)

            def exponentials(k, bank, count):
                act.wait_ge(s["bias_" + k], count)
                for t in range(NT):
                    ins = act.activation(probs[k][:, t, :], bank[:, t * K:(t + 1) * K], ACT.Exp, scale=SCALE,
                                         bias=exp_bias[k][:, t:t + 1], accum_out=row_sum[k][:, t:t + 1])
                ins.then_inc(s["exp_" + k], 1)

            def iteration(i, stages):
                n, a, f, z = i + 1, i, i - 1, i - 2
                if "A" in stages:
                    high_q("a", A0, a + 1)
                if "F" in stages:
                    act.wait_ge(s["o_offset_ready"], f + 1)
                    for t in range(NT):
                        ins = act.activation(o_hat[:, t, :], o[:, t, :], ACT.Identity, bias=o_offset[:, t:t + 1],
                                             scale=o_rstd[:, t:t + 1])
                    ins.then_inc(s["o_hat_ready"], 1)
                if "Z" in stages:
                    high(flat(cT["1"], HI), F0, "c_1", z + 1)
                if "A" in stages:
                    act.wait_ge(s["a_hat_ready"], a + 1)
                    act.wait_ge(s["c_a_done"], a)
                    act.copy(flat(rows["a"], HI), a_hat[:, :, :].rearrange("p c l -> p (c l)")).then_inc(s["rows_a_high"], 1)
                    act.wait_ge(s["v_hat_ready"], a + 1)
                    act.wait_ge(s["c_v_done"], a)
                    act.copy(flat(rows["v"], HI), v_hat[:, :, :].rearrange("p c l -> p (c l)")).then_inc(s["rows_v_high"], 1)
                    high_q("v", A1, a + 1)
                if "F" in stages:
                    high(halves(oT, HI, 0), F1, "oT0", f + 1)
                    high(halves(oT, HI, 1), F2, "oT1", f + 1)
                    act.wait_ge(s["ctx1_loaded"], 16 * (f + 1))
                    act.wait_ge(s["c_1_done"], f)
                    act.copy(flat(rows["1"], HI), ctx1_in[:, :, :].rearrange("p c l -> p (c l)")).then_inc(s["rows_1_high"], 1)
                if "A" in stages:
                    exponentials("a", A2, a + 1)
                    exponentials("v", A0, a + 1)
                if "F" in stages:
                    act.wait_ge(s["ctxT1_loaded"], 16 * (f + 1))
                    act.wait_ge(s["s_1_done"], f)
                    act.copy(flat(kT["1"], HI), ctxT1_in[:, :, :].rearrange("p c l -> p (c l)")).then_inc(s["kT_1_high"], 1)
                if "A" in stages:
                    high(flat(pT["a"], HI), A1, "pT_a", a + 1)
                    high(flat(pT["v"], HI), A2, "pT_v", a + 1)
                if "N" in stages:
                    high(halves(xT, HI, 0), N0, "xT0", n + 1)
                    high(halves(xT, HI, 1), N1, "xT1", n + 1)
                if "F" in stages:
                    high(halves(yT, HI, 0), F1, "yT0", f + 1)
                    high(halves(yT, HI, 1), F2, "yT1", f + 1)
                if "A" in stages:
                    high(flat(cT["a"], HI), A0, "c_a", a + 1)
                    high(flat(cT["v"], HI), A1, "c_v", a + 1)
                if "F" in stages:
                    high_q("1", F0, f + 1)
                    exponentials("1", F1, f + 1)
                if "N" in stages:
                    high(flat(kT["a"], HI), N0, "kT_a", n + 1)
                    high(flat(kT["v"], HI), N1, "kT_v", n + 1)
                if "F" in stages:
                    high(flat(pT["1"], HI), F2, "pT_1", f + 1)

            all_iterations(act, iteration)

        @block.vector
        def _(dve):
            def low(target, source, high, name, count):
                dve.wait_ge(s[name + "_high"], count)
                dve.tensor_tensor(target, source, high, ALU.subtract).then_inc(s[name + "_split"], 1)

            def low_q(k, bank, count):
                dve.wait_ge(s[f"q_{k}_high"], count)
                for j in range(NC):
                    ins = dve.scalar_tensor_tensor(out=qT[k][:, LO, j, :], in0=bank[:, j * L:(j + 1) * L],
                                                   scalar=m[k][:, j:j + 1], in1=qT[k][:, HI, j, :],
                                                   op0=ALU.add, op1=ALU.subtract)
                ins.then_inc(s[f"q_{k}_split"], 1)

            def softmax_bias(k, bank, count):
                dve.wait_ge(s[f"s_{k}_done"], count)
                dve.tensor_reduce(top[k][:, :], bank[:, :].rearrange("p (t l) -> p t l", t=NT), AX.X,
                                  ALU.max).then_inc(s["top_" + k], 1)
                dve.wait_ge(s["top_" + k], count)
                dve.scalar_tensor_tensor(out=total[k][:, :], in0=top[k][:, :], scalar=SCALE, in1=shift[k][:, :],
                                         op0=ALU.mult, op1=ALU.add).then_inc(s["total_" + k], 1)
                dve.wait_ge(s["total_" + k], count)
                dve.tensor_tensor(exp_bias[k][:, :], shift[k][:, :], total[k][:, :],
                                  ALU.subtract).then_inc(s["bias_" + k], 1)

            def weigh(k, count):
                dve.wait_ge(s["exp_" + k], count)
                dve.reciprocal(inverse[k][:, :], row_sum[k][:, :]).then_inc(s["inverse_" + k], 1)
                dve.wait_ge(s["inverse_" + k], count)
                for t in range(NT):
                    ins = dve.tensor_scalar(probs[k][:, t, :], probs[k][:, t, :], inverse[k][:, t:t + 1], None, ALU.mult)
                ins.then_inc(s["probs_" + k], 1)

            def add_shift(k, source):
                for t in range(NT):
                    ins = dve.tensor_tensor_reduce(product[:, t, :], source[:, t, :], u[k][:, :], SCALE, u0[k][:, 0:1],
                                                   ALU.mult, ALU.add, shift[k][:, t:t + 1])
                return ins

            def iteration(i, stages):
                n, a, f, z = i + 1, i, i - 1, i - 2
                if "A" in stages:
                    low_q("a", A0, a + 1)
                if "Z" in stages:
                    low(flat(cT["1"], LO), F0[:, :], flat(cT["1"], HI), "c_1", z + 1)
                if "N" in stages:
                    dve.wait_ge(s["ctx_loaded"], 16 * (n + 1))
                    for t in range(NK):
                        dve.bn_stats(stats[:, NT + t, :], ctx_in[:, t, :])
                    dve.wait_ge(s["fside_loaded"], 16 * (n + 1))
                    for t in range(NK):
                        dve.bn_stats(stats[:, NT + NK + t, :], fside_in[:, t, :])
                if "A" in stages:
                    low_q("v", A1, a + 1)
                if "F" in stages:
                    low(halves(oT, LO, 0), F1[:, :], halves(oT, HI, 0), "oT0", f + 1)
                    low(halves(oT, LO, 1), F2[:, :], halves(oT, HI, 1), "oT1", f + 1)
                if "N" in stages:
                    dve.wait_ge(s["x_loaded"], 16 * (n + 1))
                    for t in range(NT):
                        ins = dve.bn_stats(stats[:, t, :], x_in[:, t, :])
                    ins.then_inc(s["stats_ready"], 1)
                if "Z" in stages:
                    dve.wait_ge(s["y_bias_ready"], z + 1)
                    dve.wait_ge(s["z0_done"], z + 1)
                    dve.tensor_tensor(y[:, 0, :], N0[:, :], y[:, 0, :], ALU.add).then_inc(s["z0_ready"], 1)
                if "N" in stages:
                    dve.wait_ge(s["stats_ready"], 1)
                    dve.wait_ge(s["stats_ready"], n + 1)
                    dve.wait_ge(s["v_hat_ready"], n)
                    for j in range(NS):
                        ins = dve.bn_aggr(moments[:, j, :], stats[:, j, :])
                    ins.then_inc(s["moments_ready"], 1)
                if "N" in stages:
                    dve.wait_ge(s["moments_ready"], n + 1)
                    dve.tensor_scalar(neg_mean[:, :], moments[:, :, 0], -1.0, None, ALU.mult)
                    dve.tensor_scalar(var[:, :], moments[:, :, 1], EPS, None, ALU.add).then_inc(s["var_ready"], 1)
                if "Z" in stages:
                    dve.wait_ge(s["z1_done"], z + 1)
                    dve.tensor_tensor(y[:, 1, :], N1[:, :], y[:, 1, :], ALU.add).then_inc(s["z1_ready"], 1)
                if "A" in stages:
                    softmax_bias("a", A2, a + 1)
                    softmax_bias("v", A0, a + 1)
                    weigh("a", a + 1)
                    weigh("v", a + 1)
                if "F" in stages:
                    dve.wait_ge(s["o_bias_ready"], f + 1)
                    dve.wait_ge(s["fc0_done"], f + 1)
                    dve.wait_ge(s["out0_stored"], 16 * f)
                    dve.tensor_tensor(y[:, 0, :], F2[:, :], o[:, 0, :], ALU.add).then_inc(s["y0_ready"], 1)
                if "N" in stages:
                    dve.wait_ge(s["x_hat_ready"], n + 1)
                    if "F" in stages:
                        dve.wait_ge(s["shift_1"], f)
                    add_shift("a", x_hat).then_inc(s["shift_a"], 1)
                if "F" in stages:
                    dve.wait_ge(s["fc1_done"], f + 1)
                    dve.wait_ge(s["out1_stored"], 16 * f)
                    dve.tensor_tensor(y[:, 1, :], F0[:, :], o[:, 1, :], ALU.add).then_inc(s["y1_ready"], 1)
                if "A" in stages:
                    low(flat(pT["a"], LO), A1[:, :], flat(pT["a"], HI), "pT_a", a + 1)
                    low(flat(pT["v"], LO), A2[:, :], flat(pT["v"], HI), "pT_v", a + 1)
                if "N" in stages:
                    low(halves(xT, LO, 0), N0[:, :], halves(xT, HI, 0), "xT0", n + 1)
                    low(halves(xT, LO, 1), N1[:, :], halves(xT, HI, 1), "xT1", n + 1)
                if "F" in stages:
                    low(halves(yT, LO, 0), F1[:, :], halves(yT, HI, 0), "yT0", f + 1)
                    low(halves(yT, LO, 1), F2[:, :], halves(yT, HI, 1), "yT1", f + 1)
                if "N" in stages:
                    dve.wait_ge(s["shift_a"], n + 1)
                    add_shift("v", x_hat).then_inc(s["shift_v"], 1)
                if "A" in stages:
                    low(flat(cT["a"], LO), A0[:, :], flat(cT["a"], HI), "c_a", a + 1)
                    low(flat(cT["v"], LO), A1[:, :], flat(cT["v"], HI), "c_v", a + 1)
                if "F" in stages:
                    dve.wait_ge(s["y1_ready"], f + 1)
                    if "N" in stages:
                        dve.wait_ge(s["shift_v"], n + 1)
                    add_shift("1", y).then_inc(s["shift_1"], 1)
                    low_q("1", F0, f + 1)
                if "A" in stages:
                    dve.wait_ge(s["x_bias_ready"], a + 1)
                    dve.wait_ge(s["attn0_done"], a + 1)
                    dve.tensor_tensor(o[:, 0, :], A2[:, :], x_bias[:, 0, :], ALU.add).then_inc(s["o0_ready"], 1)
                if "F" in stages:
                    dve.wait_ge(s["shift_1"], f + 1)
                    softmax_bias("1", F1, f + 1)
                if "A" in stages:
                    dve.wait_ge(s["o0_ready"], a + 1)
                    dve.bn_stats(o_stats[:, 0, :], o[:, 0, :])
                if "F" in stages:
                    weigh("1", f + 1)
                if "A" in stages:
                    dve.wait_ge(s["attn1_done"], a + 1)
                    dve.tensor_tensor(o[:, 1, :], A1[:, :], x_bias[:, 1, :], ALU.add).then_inc(s["o1_ready"], 1)
                    dve.wait_ge(s["o1_ready"], a + 1)
                    dve.bn_stats(o_stats[:, 1, :], o[:, 1, :]).then_inc(s["o_stats_ready"], 1)
                    dve.wait_ge(s["o_stats_ready"], 1)
                    dve.wait_ge(s["o_stats_ready"], a + 1)
                    for t in range(NT):
                        ins = dve.bn_aggr(o_moments[:, t, :], o_stats[:, t, :])
                    ins.then_inc(s["o_moments_ready"], 1)
                    dve.wait_ge(s["o_moments_ready"], a + 1)
                    dve.tensor_scalar(o_neg_mean[:, :], o_moments[:, :, 0], -1.0, None, ALU.mult)
                    dve.tensor_scalar(o_var[:, :], o_moments[:, :, 1], EPS, None, ALU.add).then_inc(s["o_var_ready"], 1)
                if "F" in stages:
                    low(flat(pT["1"], LO), F2[:, :], flat(pT["1"], HI), "pT_1", f + 1)
                if "N" in stages:
                    low(flat(kT["a"], LO), N0[:, :], flat(kT["a"], HI), "kT_a", n + 1)
                    low(flat(kT["v"], LO), N1[:, :], flat(kT["v"], HI), "kT_v", n + 1)

            all_iterations(dve, iteration)

        @block.gpsimd
        def _(pool):
            pool.memset(power[:, :], -0.5).then_inc(s["power_set"], 1)
            pool.wait_ge(s["power_set"], 1)

            def normalise(target, source, scale, shift, t):
                return pool.tensor_scalar(target[:, t, :], source[:, t, :], scale, shift, ALU.mult, ALU.add)

            def low(target, source, high, name, count):
                pool.wait_ge(s[name + "_high"], count)
                pool.tensor_tensor(target, source, high, ALU.subtract).then_inc(s[name + "_split"], 1)

            def iteration(i, stages):
                n, a, f, z = i + 1, i, i - 1, i - 2
                if "F" in stages:
                    pool.wait_ge(s["o_var_ready"], f + 1)
                    pool.tensor_tensor(o_rstd[:, :], o_var[:, :], power[:, 0:NT], ALU.pow).then_inc(s["o_rstd_ready"], 1)
                    pool.wait_ge(s["o_rstd_ready"], f + 1)
                    pool.tensor_tensor(o_offset[:, :], o_neg_mean[:, :], o_rstd[:, :], ALU.mult).then_inc(s["o_offset_ready"], 1)
                if "A" in stages:
                    pool.wait_ge(s["x_loaded"], 16 * (a + 1))
                    pool.wait_ge(s["o1_ready"], a)
                    for t in range(NT):
                        ins = pool.tensor_tensor(x_bias[:, t, :], x_in[:, t, :], bias_attn[:, :], ALU.add)
                    ins.then_inc(s["x_bias_ready"], 1)
                    low(flat(rows["a"], LO), a_hat[:, :, :].rearrange("p c l -> p (c l)"), flat(rows["a"], HI), "rows_a", a + 1)
                    low(flat(rows["v"], LO), v_hat[:, :, :].rearrange("p c l -> p (c l)"), flat(rows["v"], HI), "rows_v", a + 1)
                if "F" in stages:
                    pool.wait_ge(s["o_hat_ready"], f + 1)
                    for t in range(NT):
                        ins = pool.tensor_tensor(o[:, t, :], o[:, t, :], bias_fc[:, :], ALU.add)
                    ins.then_inc(s["o_bias_ready"], 1)
                    low(flat(rows["1"], LO), ctx1_in[:, :, :].rearrange("p c l -> p (c l)"), flat(rows["1"], HI), "rows_1", f + 1)
                if "N" in stages:
                    pool.wait_ge(s["var_ready"], n + 1)
                    pool.tensor_tensor(rstd[:, :], var[:, :], power[:, :], ALU.pow).then_inc(s["rstd_ready"], 1)
                    pool.wait_ge(s["rstd_ready"], n + 1)
                    pool.tensor_tensor(offset[:, :], neg_mean[:, :], rstd[:, :], ALU.mult).then_inc(s["offset_ready"], 1)
                    pool.wait_ge(s["power_set"], 1)
                    pool.wait_ge(s["offset_ready"], n + 1)
                    pool.wait_ge(s["xT1_done"], n)
                    pool.wait_ge(s["shift_v"], n)
                    for t in range(NT):
                        ins = normalise(x_hat, x_in, rstd[:, t:t + 1], offset[:, t:t + 1], t)
                    ins.then_inc(s["x_hat_ready"], 1)
                    pool.wait_ge(s["power_set"], 1)
                    pool.wait_ge(s["rows_a_split"], n)
                    pool.wait_ge(s["kT_a_done"], n)
                    for t in range(NK):
                        ins = normalise(a_hat, ctx_in, rstd[:, NT + t:NT + t + 1], offset[:, NT + t:NT + t + 1], t)
                    ins.then_inc(s["a_hat_ready"], 1)
                    pool.wait_ge(s["power_set"], 1)
                    pool.wait_ge(s["rows_v_split"], n)
                    pool.wait_ge(s["kT_v_done"], n)
                    for t in range(NK):
                        ins = normalise(v_hat, fside_in, rstd[:, NT + NK + t:NT + NK + t + 1],
                                        offset[:, NT + NK + t:NT + NK + t + 1], t)
                    ins.then_inc(s["v_hat_ready"], 1)
                if "F" in stages:
                    low(flat(kT["1"], LO), ctxT1_in[:, :, :].rearrange("p c l -> p (c l)"), flat(kT["1"], HI), "kT_1", f + 1)
                    pool.wait_ge(s["yT1_done"], f + 1)
                    pool.wait_ge(s["shift_1"], f + 1)
                    for t in range(NT):
                        ins = pool.tensor_tensor(y[:, t, :], y[:, t, :], bias_1[:, :], ALU.add)
                    ins.then_inc(s["y_bias_ready"], 1)

            all_iterations(pool, iteration)


def kernel(**inputs):
    import numpy as np
    import concourse.bacc as bacc
    from concourse.bass_utils import run_bass_kernel_spmd

    nc = bacc.Bacc("TRN2", target_bir_lowering=False, num_devices=1)
    arrays = {}

    def dram(name, a):
        arrays[name] = np.ascontiguousarray(a)
        return nc.dram_tensor(name, arrays[name].shape, mybir.dt.from_np(arrays[name].dtype), kind="ExternalInput").ap()

    prefix = {"a": "L0_xattn_a_", "v": "L0_xattn_v_", "1": "L1_xattn_"}
    source = {"ln1_g": "g1", "ln1_b": "b1", "ln2_g": "g2", "ln2_b": "b2"}
    named = {f"{k}_{source.get(name, name)}": np.asarray(inputs[prefix[k] + name])
             for k in "av1" for name in (*source, "bq", "bk", "bv", "bo") if prefix[k] + name in inputs}
    named |= {name: np.asarray(inputs["L0_xattn_" + name]) for name in ("ln_g", "ln_b", "fc_b")}

    vectors = dram("vectors", np.concatenate([named[n].reshape(-1, P).T for n, _ in VECTORS], axis=1))
    rows = {n: dram("row_" + n, named[n]) for n, _ in ROWS}
    weights = {}
    for k in "av1":
        Wq, Wk, Wv, Wo = (np.asarray(inputs[prefix[k] + n]) for n in ("Wq", "Wk", "Wv", "Wo"))
        own = {"WqT": Wq.T, "WkT": Wk.T, "WvT": Wv.T, "Wo": Wo}
        if k != "1":
            own |= {"Wk": Wk, "Wv": Wv}
        weights[k] = {n: dram(f"{n}_{k}", w) for n, w in own.items()}
    x = dram("x", inputs["x"])
    ctx = dram("ctx", inputs["ctx_512"])
    ctxT = dram("ctxT", np.asarray(inputs["ctx_512"]).transpose(0, 2, 1))
    fside = dram("fside", inputs["fside_BxSxS_0"])
    fc_W = dram("fc_W", inputs["L0_xattn_fc_W"])
    out = nc.dram_tensor("out", x.shape, F32, kind="ExternalOutput").ap()
    build_kernel(nc, x, ctx, ctxT, fside, vectors, rows, weights, fc_W, out)
    result = run_bass_kernel_spmd(nc, [arrays], core_ids=[0])
    return result.results[0]["out"]
```

```python
from contextlib import ExitStack

import concourse.bass as bass
from concourse import mybir

F32 = mybir.dt.float32
F32R = mybir.dt.float32r
ALU = mybir.AluOpType
ACT = mybir.ActivationFunctionType
AX = mybir.AxisListType

P = 128
EPS = 1e-5
HI, LO = 0, 1

VECTORS = [(f"{k}_{name}", width) for k in ("a", "v")
           for name, width in (("g1", 512), ("g2", 256), ("bq", 512), ("bk", 512), ("bv", 512))]
VECTORS += [("1_bq", 512), ("1_bk", 512), ("1_bv", 512), ("ln_g", 512), ("ln_b", 512)]
ROWS = [("a_b1", 512), ("a_b2", 256), ("a_g1", 512), ("a_g2", 256), ("v_b1", 512), ("v_b2", 256), ("v_g1", 512),
        ("v_g2", 256), ("a_bo", 512), ("v_bo", 512), ("fc_b", 512), ("1_bo", 512)]


def build_kernel(nc, x, ctx, ctxT, fside, vectors, rows, weights, fc_W, out):
    B, L, D = x.shape
    K, C = ctx.shape[1:]
    E = weights["a"]["Wo"].shape[0]
    NT, NK, ND, NC, NE = L // P, K // P, D // P, C // P, E // P
    SCALE = float(E) ** -0.5
    ATT = ("a", "v", "1")
    assert NT * C == 512 and NC * L == 512 and NK * L == 512 and D == 512 and E == 512

    vector_at, at = {}, 0
    for name, width in VECTORS:
        vector_at[name] = (at, width // P)
        at += width // P
    n_columns = at

    with ExitStack() as stack:
        def sb(name, shape, dt=F32, on=stack):
            return on.enter_context(nc.sbuf_tensor("t_" + name, shape, dt))

        def sem(name):
            return stack.enter_context(nc.semaphore(name))

        M = {k: sb(f"M_{k}", [P, 2, ND, C], F32R) for k in ATT}
        Wvo = {k: sb(f"Wvo_{k}", [P, 2, NC, D], F32R) for k in ATT}
        Wfc = sb("Wfc", [P, 2, ND, D], F32R)
        m = {k: sb(f"m_{k}", [P, NC]) for k in ATT}
        u = {k: sb(f"u_{k}", [P, D]) for k in ATT}
        u0 = {k: sb(f"u0_{k}", [P, 1]) for k in ATT}
        bias_attn = sb("bias_attn", [P, D])
        bias_fc = sb("bias_fc", [P, D])
        bias_1 = sb("bias_1", [P, D])
        ident = sb("ident", [P, P])
        banks = [stack.enter_context(nc.psum_tensor(f"bank{j}", [P, 512], F32)) for j in range(8)]

        x_in, x_hat = (sb(n, [P, NT, D]) for n in ("x_in", "x_hat"))
        ctx_in, fside_in, ctx1_in, a_hat, v_hat = (
            sb(n, [P, NK, C]) for n in ("ctx_in", "fside_in", "ctx1_in", "a_hat", "v_hat"))
        ctxT1_in = sb("ctxT1_in", [P, NC, K])
        xT = sb("xT", [P, 2, ND, L], F32R)
        kT = {k: sb(f"kT_{k}", [P, 2, NC, K], F32R) for k in "av"}
        o_hat = sb("o_hat", [P, NT, D])
        shift, top, total, exp_bias, row_sum, inverse = (
            {k: sb(f"{n}_{k}", [P, NT]) for k in "av1"}
            for n in ("shift", "top", "total", "exp_bias", "row_sum", "inverse"))
        NS = 3 * 2
        stats, moments = sb("stats", [P, NS, 6]), sb("moments", [P, NS, 2])
        var, rstd, neg_mean, offset = (sb(n, [P, NS]) for n in ("var", "rstd", "neg_mean", "offset"))
        o_stats, o_moments = sb("o_stats", [P, NT, 6]), sb("o_moments", [P, NT, 2])
        o_var, o_rstd, o_neg_mean, o_offset = (sb(n, [P, NT]) for n in ("o_var", "o_rstd", "o_neg_mean", "o_offset"))
        power = sb("power", [P, NS])
        ones = sb("ones", [P, P])
        cols = sb("cols", [P, n_columns])
        kb, vb, qb = ({k: sb(f"{n}_{k}", [P, NE]) for k in ("a", "v")} for n in ("kb", "vb", "qb"))
        qk = {k: sb(f"qk_{k}", [P, 1]) for k in ATT}


        with ExitStack() as folding:
            raw_fc = sb("raw_fc", [P, ND, D], on=folding)
            row_part, row_term = sb("row_part", [P, D], on=folding), sb("row_term", [P, 2, D], on=folding)
            row = {n: sb(f"row_{n}", [P, width], on=folding) for n, width in ROWS
                   if n[2:] in ("b1", "b2", "g2") or n == "v_bo"}
            raw = [dict(WqT=sb(f"WqT{j}", [P, NE, D], on=folding), WkT=sb(f"WkT{j}", [P, NE, C], on=folding),
                        WvT=sb(f"WvT{j}", [P, NE, C], on=folding), Wo=sb(f"Wo{j}", [P, NE, D], on=folding))
                   for j in range(2)]
            M_full = sb("M_full", [P, ND, C], on=folding)
            O_full = sb("O_full", [P, NC, D], on=folding)
            terms = sb("terms", [P, NE, 256], on=folding)
            u_part = sb("u_part", [P, D], on=folding)
            m_part, m_term = (sb(n, [P, C], on=folding) for n in ("m_part", "m_term"))

        y = sb("y", [P, NT, D])
        yT, oT = (sb(n, [P, 2, ND, L], F32R) for n in ("yT", "oT"))
        x_bias, o = (sb(n, [P, NT, D]) for n in ("x_bias", "o"))
        kT["1"] = sb("kT_1", [P, 2, NC, K], F32R)
        rows_split, qT, pT, cT = ({k: sb(f"{n}_{k}", [P, 2, 2, 256], F32R) for k in "av1"}
                                  for n in ("rows", "qT", "pT", "cT"))
        probs = {k: sb(f"probs_{k}", [P, NT, K]) for k in "av1"}

        A0, A1, A2, F0, F1, F2, N0, N1 = banks

        names = """
            x_loaded ctx_loaded fside_loaded ctx1_loaded ctxT1_loaded out0_stored out1_stored
            q_a_done q_v_done q_1_done s_a_done s_v_done s_1_done pT_a_done pT_v_done pT_1_done
            c_a_done c_v_done c_1_done xT0_done xT1_done oT0_done oT1_done yT0_done yT1_done
            kT_a_done kT_v_done attn0_done attn1_done fc0_done fc1_done z0_done z1_done
            q_a_high q_v_high q_1_high pT_a_high pT_v_high pT_1_high c_a_high c_v_high c_1_high
            xT0_high xT1_high oT0_high oT1_high yT0_high yT1_high kT_a_high kT_v_high kT_1_high
            rows_a_high rows_v_high rows_1_high
            q_a_split q_v_split q_1_split pT_a_split pT_v_split pT_1_split c_a_split c_v_split c_1_split
            xT0_split xT1_split oT0_split oT1_split yT0_split yT1_split kT_a_split kT_v_split kT_1_split
            rows_a_split rows_v_split rows_1_split
            top_a top_v top_1 bias_a bias_v bias_1 exp_a exp_v exp_1
            inverse_a inverse_v inverse_1 probs_a probs_v probs_1 shift_a shift_v shift_1
            stats_ready moments_ready var_ready rstd_ready o_stats_ready o_moments_ready o_var_ready
            o_rstd_ready offset_ready o_offset_ready x_hat_ready a_hat_ready v_hat_ready o_hat_ready x_bias_ready o_bias_ready
            y_bias_ready o0_ready o1_ready y1_ready z0_ready z1_ready power_set
        """.split()
        names += [f"qk_weights_{k}" for k in ATT] + [f"vo_weights_{k}" for k in ATT]
        names += """
            Wq_rest_loaded columns_loaded rows_a_loaded rows_v_loaded biases_loaded fc_loaded ident_ready ones_ready
            G_done H_done u_done m_done row_done kb_ready qb_half qb_ready vb_ready qk_ready
            u_step row_added M_scaled M_high M_split O_scaled O_high O_split
            u_copied m_copied row_copied row_scaled row_step m_step fc_high fc_split fc_row_step
        """.split()
        s = {n: sem(n) for n in names}

        def column(name, j=None):
            at, width = vector_at[name]
            return cols[:, at:at + width] if j is None else cols[:, at + j:at + j + 1]

        def kbias(k):
            return kb[k] if k in kb else column(k + "_bk")

        def qbias(k):
            return qb[k] if k in qb else column(k + "_bq")

        def vbias(k):
            return vb[k] if k in vb else column(k + "_bv")

        G_bank, H_bank, u_bank, small_bank = banks[0:2], banks[2:4], banks[4], banks[5]
        row_bank = {"a": banks[6], "v": banks[6], "1": banks[7]}
        fc_row_bank = banks[3]

        x_rows = x.rearrange("b (t p) d -> b p t d", p=P)
        ctx_rows = ctx.rearrange("b (t p) d -> b p t d", p=P)
        ctxT_rows = ctxT.rearrange("b (t p) d -> b p t d", p=P)
        fside_rows = fside.rearrange("b (t p) d -> b p t d", p=P)
        out_rows = out.rearrange("b (t p) d -> b p t d", p=P)

        STEPS, SUM_STEPS = NE - 1, 2 * (NE - 1)
        block = stack.enter_context(nc.Block())

        HEAD = [(-1, "N"), (-1, "T"), (0, "NTA"), (1, "NTAF")]
        TAIL = [(B - 1, "AFZ"), (B, "FZ"), (B + 1, "Z")]

        def whole_program(engine, fold, iteration, folded=lambda: None):
            fold(0, "a")
            fold(1, "v")
            iteration(*HEAD[0])
            fold(3, "fc")
            fold(2, "1")
            iteration(*HEAD[1])
            folded()
            iteration(*HEAD[2])
            fold(3, "fc bias")
            iteration(*HEAD[3])
            with engine.Fori(2, B - 1) as i:
                iteration(i, "NTAFZ")
            for i, stages in TAIL:
                iteration(i, stages)

        @block.sync
        def _(sp):
            def load_weights(n, k, names, sem_name):
                for name in names:
                    sp.dma_start(raw[n % 2][name][:, :, :],
                                 weights[k][name].rearrange("(c p) n -> p c n", p=P)).then_inc(s[sem_name], 16)

            def spread_row(target, name, sem_name):
                sp.dma_start(target[:, :], rows[name].partition_broadcast(P)).then_inc(s[sem_name], 16)

            def fold(n, k):
                if n == 0:
                    load_weights(n, k, ("WkT",), "qk_weights_a")
                    for half, sem_name in ((0, "qk_weights_a"), (1, "Wq_rest_loaded")):
                        part = slice(half * D // 2, (half + 1) * D // 2)
                        sp.dma_start(raw[0]["WqT"][:, :, part],
                                     weights[k]["WqT"].rearrange("(c p) n -> p c n", p=P)[:, :, part]).then_inc(s[sem_name], 16)
                if n == 1:
                    load_weights(n, k, ("WkT", "WqT"), "qk_weights_" + k)
                if n == 0:
                    sp.dma_start(cols[:, :], vectors).then_inc(s["columns_loaded"], 16)
                if n < 2:
                    for name in ("b2", "b1", "g2"):
                        spread_row(row[f"{k}_{name}"], f"{k}_{name}", f"rows_{k}_loaded")
                    spread_row(u[k], k + "_g1", f"rows_{k}_loaded")
                    load_weights(n, k, ("WvT", "Wo"), "vo_weights_" + k)
                if n == 1:
                    for target, name in ((bias_attn, "a_bo"), (row["v_bo"], "v_bo"), (bias_1, "1_bo"), (bias_fc, "fc_b")):
                        spread_row(target, name, "biases_loaded")
                    sp.dma_start(raw_fc[:, :, :], fc_W.rearrange("(c p) n -> p c n", p=P)).then_inc(s["fc_loaded"], 16)
                if n == 2:
                    sp.wait_ge(s["G_done"], 1)
                    sp.wait_ge(s["u_step"], NE)
                    sp.wait_ge(s["m_step"], SUM_STEPS)
                    load_weights(n, k, ("WqT", "WkT"), "qk_weights_1")
                    sp.wait_ge(s["H_done"], 1)
                    sp.wait_ge(s["row_step"], STEPS)
                    load_weights(n, k, ("WvT", "Wo"), "vo_weights_1")

            def iteration(i, stages):
                n, a, f, z = i + 1, i, i - 1, i - 2
                if "F" in stages:
                    sp.wait_ge(s["rows_1_split"], f)
                    sp.dma_start(ctx1_in[:, :, :], ctx_rows[f]).then_inc(s["ctx1_loaded"], 16)
                    sp.wait_ge(s["kT_1_split"], f)
                    sp.dma_start(ctxT1_in[:, :, :], ctxT_rows[f]).then_inc(s["ctxT1_loaded"], 16)
                if "N" in stages:
                    sp.wait_ge(s["a_hat_ready"], n)
                    sp.dma_start(ctx_in[:, :, :], ctx_rows[n]).then_inc(s["ctx_loaded"], 16)
                    sp.wait_ge(s["v_hat_ready"], n)
                    sp.dma_start(fside_in[:, :, :], fside_rows[n]).then_inc(s["fside_loaded"], 16)
                    sp.wait_ge(s["x_bias_ready"], n)
                    sp.dma_start(x_in[:, :, :], x_rows[n]).then_inc(s["x_loaded"], 16)
                if "Z" in stages:
                    sp.wait_ge(s["z0_ready"], z + 1)
                    sp.dma_start(out_rows[z, :, 0], y[:, 0, :]).then_inc(s["out0_stored"], 16)
                    sp.wait_ge(s["z1_ready"], z + 1)
                    sp.dma_start(out_rows[z, :, 1], y[:, 1, :]).then_inc(s["out1_stored"], 16)

            whole_program(sp, fold, iteration)
            sp.wait_ge(s["out0_stored"], 16 * B)
            sp.wait_ge(s["out1_stored"], 16 * B)

        @block.tensor
        def _(pe):
            def product3(out, left, right, chunks):
                passes = [(h, g) for h, g in ((HI, HI), (HI, LO), (LO, HI))]
                for c in range(chunks):
                    for h, g in passes:
                        mm = pe.matmul(out, left(h, c), right(g, c), start=c == 0 and (h, g) == (HI, HI),
                                       stop=c == chunks - 1 and (h, g) == (LO, HI))
                return mm

            def project(bank, k, source):
                for j in range(NC):
                    mm = product3(bank[:, j * L:(j + 1) * L], lambda h, c: M[k][:, h, c, j * P:(j + 1) * P],
                                  lambda g, c: source[:, g, c, :], ND)
                return mm

            def scores(bank, k):
                for t in range(NT):
                    mm = product3(bank[:, t * K:(t + 1) * K], lambda h, c: qT[k][:, h, c, t * P:(t + 1) * P],
                                  lambda g, c: kT[k][:, g, c, :], NC)
                return mm

            def turn(bank, blocks):
                for j, b in enumerate(blocks):
                    mm = pe.transpose(bank[:, j * P:(j + 1) * P], b, ident[:, :])
                return mm

            def turned_probs(k):
                return [probs[k][:, t, c * P:(c + 1) * P] for c in range(NK) for t in range(NT)]

            def mix(bank, k):
                for j in range(NC):
                    mm = product3(bank[:, j * L:(j + 1) * L], lambda h, c: rows_split[k][:, h, c, j * P:(j + 1) * P],
                                  lambda g, c: pT[k][:, g, c, :], NK)
                return mm

            def turned(tile, half):
                return [tile[:, t, c * P:(c + 1) * P] for c in (2 * half, 2 * half + 1) for t in range(NT)]

            def attention_out(bank, t):
                for k in "av":
                    for c in range(NC):
                        for h, g in ((HI, HI), (HI, LO), (LO, HI)):
                            mm = pe.matmul(bank[:, :], cT[k][:, h, c, t * P:(t + 1) * P], Wvo[k][:, g, c, :],
                                           start=k == "a" and c == 0 and (h, g) == (HI, HI),
                                           stop=k == "v" and c == NC - 1 and (h, g) == (LO, HI))
                return mm

            def iteration(i, stages):
                n, a, f, z = i + 1, i, i - 1, i - 2
                if "A" in stages:
                    pe.wait_ge(s["xT0_split"], a + 1)
                    pe.wait_ge(s["xT1_split"], a + 1)
                    project(A0, "a", xT).then_inc(s["q_a_done"], 1)
                if "Z" in stages:
                    pe.wait_ge(s["rows_1_split"], z + 1)
                    pe.wait_ge(s["pT_1_split"], z + 1)
                    mix(F0, "1").then_inc(s["c_1_done"], 1)
                if "A" in stages:
                    pe.wait_ge(s["o1_ready"], a)
                    project(A1, "v", xT).then_inc(s["q_v_done"], 1)
                if "F" in stages:
                    pe.wait_ge(s["o_hat_ready"], f + 1)
                    pe.wait_ge(s["exp_1"], f)
                    turn(F1, turned(o_hat, 0)).then_inc(s["oT0_done"], 1)
                    pe.wait_ge(s["pT_1_split"], f)
                    turn(F2, turned(o_hat, 1)).then_inc(s["oT1_done"], 1)
                if "Z" in stages:
                    pe.wait_ge(s["c_1_split"], z + 1)
                    if "A" in stages:
                        pe.wait_ge(s["kT_a_split"], a + 1)
                        pe.wait_ge(s["kT_v_split"], a + 1)
                    product3(N0[:, :], lambda h, c: cT["1"][:, h, c, 0:P],
                             lambda g, c: Wvo["1"][:, g, c, :], NC).then_inc(s["z0_done"], 1)
                    product3(N1[:, :], lambda h, c: cT["1"][:, h, c, P:2 * P],
                             lambda g, c: Wvo["1"][:, g, c, :], NC).then_inc(s["z1_done"], 1)
                if "A" in stages:
                    pe.wait_ge(s["q_a_split"], a + 1)
                    pe.wait_ge(s["kT_a_split"], a + 1)
                    pe.wait_ge(s["o0_ready"], a)
                    scores(A2, "a").then_inc(s["s_a_done"], 1)
                    pe.wait_ge(s["q_v_split"], a + 1)
                    pe.wait_ge(s["kT_v_split"], a + 1)
                    scores(A0, "v").then_inc(s["s_v_done"], 1)
                if "F" in stages:
                    pe.wait_ge(s["oT0_split"], f + 1)
                    pe.wait_ge(s["oT1_split"], f + 1)
                    product3(F2[:, :], lambda h, c: oT[:, h, c, 0:P],
                             lambda g, c: Wfc[:, g, c, :], ND).then_inc(s["fc0_done"], 1)
                    product3(F0[:, :], lambda h, c: oT[:, h, c, P:2 * P],
                             lambda g, c: Wfc[:, g, c, :], ND).then_inc(s["fc1_done"], 1)
                if "A" in stages:
                    pe.wait_ge(s["probs_a"], a + 1)
                    turn(A1, turned_probs("a")).then_inc(s["pT_a_done"], 1)
                    pe.wait_ge(s["probs_v"], a + 1)
                    turn(A2, turned_probs("v")).then_inc(s["pT_v_done"], 1)
                if "T" in stages:
                    pe.wait_ge(s["ident_ready"], 2)
                    pe.wait_ge(s["x_hat_ready"], n + 1)
                    if "Z" in stages:
                        pe.wait_ge(s["z0_ready"], z + 1)
                        pe.wait_ge(s["z1_ready"], z + 1)
                    turn(N0, turned(x_hat, 0)).then_inc(s["xT0_done"], 1)
                    pe.wait_ge(s["row_copied"], 2)
                    turn(N1, turned(x_hat, 1)).then_inc(s["xT1_done"], 1)
                if "F" in stages:
                    pe.wait_ge(s["y1_ready"], f + 1)
                    turn(F1, turned(y, 0)).then_inc(s["yT0_done"], 1)
                    turn(F2, turned(y, 1)).then_inc(s["yT1_done"], 1)
                if "A" in stages:
                    pe.wait_ge(s["rows_a_split"], a + 1)
                    pe.wait_ge(s["pT_a_split"], a + 1)
                    mix(A0, "a").then_inc(s["c_a_done"], 1)
                    pe.wait_ge(s["rows_v_split"], a + 1)
                    pe.wait_ge(s["pT_v_split"], a + 1)
                    mix(A1, "v").then_inc(s["c_v_done"], 1)
                if "F" in stages:
                    pe.wait_ge(s["yT0_split"], f + 1)
                    pe.wait_ge(s["yT1_split"], f + 1)
                    project(F0, "1", yT).then_inc(s["q_1_done"], 1)
                if "A" in stages:
                    pe.wait_ge(s["c_a_split"], a + 1)
                    pe.wait_ge(s["c_v_split"], a + 1)
                    attention_out(A2, 0).then_inc(s["attn0_done"], 1)
                if "F" in stages:
                    pe.wait_ge(s["q_1_split"], f + 1)
                    pe.wait_ge(s["kT_1_split"], f + 1)
                    scores(F1, "1").then_inc(s["s_1_done"], 1)
                if "A" in stages:
                    attention_out(A1, 1).then_inc(s["attn1_done"], 1)
                if "T" in stages:
                    pe.wait_ge(s["a_hat_ready"], n + 1)
                    pe.wait_ge(s["xT0_split"], n + 1)
                    turn(N0, [a_hat[:, t, c * P:(c + 1) * P] for c in range(NC) for t in range(NK)]).then_inc(s["kT_a_done"], 1)
                    pe.wait_ge(s["v_hat_ready"], n + 1)
                    pe.wait_ge(s["xT1_split"], n + 1)
                    turn(N1, [v_hat[:, t, c * P:(c + 1) * P] for c in range(NC) for t in range(NK)]).then_inc(s["kT_v_done"], 1)
                if "F" in stages:
                    pe.wait_ge(s["probs_1"], f + 1)
                    turn(F2, turned_probs("1")).then_inc(s["pT_1_done"], 1)

            def fold(n, k):
                def whole(out, left, right):
                    for e in range(NE):
                        mm = pe.matmul(out, left(e), right(e), start=e == 0, stop=e == NE - 1)
                    return mm

                if k == "fc":
                    return
                if k == "fc bias":
                    pe.wait_ge(s["fc_row_step"], SUM_STEPS)
                    pe.matmul(fc_row_bank[:, :], ones[:, :], row_part[:, :], start=True, stop=True).then_inc(s["row_done"], 1)
                    pe.wait_ge(s["fc_split"], 1)
                    return
                w = raw[n % 2]
                pe.wait_ge(s["qk_weights_" + k], 32)
                pe.wait_ge(s["M_split"], n)
                for i in range(ND):
                    if n == 0 and i == ND // 2:
                        pe.wait_ge(s["Wq_rest_loaded"], 16)
                    mm = whole(G_bank[i // 2][:, (i % 2) * C:(i % 2 + 1) * C],
                               lambda e: w["WqT"][:, e, i * P:(i + 1) * P], lambda e: w["WkT"][:, e, :])
                mm.then_inc(s["G_done"], 1)
                pe.wait_ge(s["vo_weights_" + k], 32)
                pe.wait_ge(s["O_scaled"], n)
                for j in range(NC):
                    mm = whole(H_bank[j][:, :], lambda e: w["WvT"][:, e, j * P:(j + 1) * P], lambda e: w["Wo"][:, e, :])
                mm.then_inc(s["H_done"], 1)
                pe.wait_ge(s["ones_ready"], 1)
                pe.wait_ge(s["u_step"], NE * (n + 1))
                pe.wait_ge(s["u_copied"], n)
                pe.matmul(u_bank[:, :], ones[:, :], u_part[:, :], start=True, stop=True).then_inc(s["u_done"], 1)
                pe.wait_ge(s["m_step"], (n + 1) * SUM_STEPS)
                pe.wait_ge(s["qk_ready"], n + 1)
                pe.wait_ge(s["m_copied"], n)
                pe.matmul(small_bank[:, NC:NC + 1], ones[:, :], qk[k][:, :], start=True, stop=True)
                for j in range(NC):
                    mm = pe.matmul(small_bank[:, j:j + 1], m_part[:, j * P:(j + 1) * P], ones[:, 0:1], start=True, stop=True)
                mm.then_inc(s["m_done"], 1)
                pe.wait_ge(s["row_step"], (n + 1) * STEPS)
                pe.matmul(row_bank[k][:, :], ones[:, :], row_part[:, :], start=k != "v", stop=k != "a").then_inc(s["row_done"], 1)
                if k == "1":
                    pe.wait_ge(s["row_copied"], 1)

            def folded():
                pe.wait_ge(s["m_copied"], 3)
                pe.wait_ge(s["u_copied"], 3)
                pe.wait_ge(s["M_split"], 3)
                pe.wait_ge(s["O_split"], 3)

            whole_program(pe, fold, iteration, folded)

        def halves(tile, part, half):
            return tile[:, part, 2 * half:2 * half + 2, :].rearrange("p c l -> p (c l)")

        def flat(tile, part):
            return tile[:, part, :, :].rearrange("p c l -> p (c l)")

        @block.scalar
        def _(act):
            def high(target, bank, name, count):
                act.wait_ge(s[name + "_done"], count)
                act.copy(target, bank[:, :]).then_inc(s[name + "_high"], 1)

            def high_q(k, bank, count):
                act.wait_ge(s[f"q_{k}_done"], count)
                act.activation(qT[k][:, HI, 0, :], bank[:, 0:L], ACT.Identity, bias=m[k][:, 0:1])
                act.activation(qT[k][:, HI, 1, :], bank[:, L:2 * L], ACT.Identity,
                               bias=m[k][:, 1:2]).then_inc(s[f"q_{k}_high"], 1)

            def exponentials(k, bank, count):
                act.wait_ge(s["bias_" + k], count)
                for t in range(NT):
                    ins = act.activation(probs[k][:, t, :], bank[:, t * K:(t + 1) * K], ACT.Exp, scale=SCALE,
                                         bias=exp_bias[k][:, t:t + 1], accum_out=row_sum[k][:, t:t + 1])
                ins.then_inc(s["exp_" + k], 1)

            def iteration(i, stages):
                n, a, f, z = i + 1, i, i - 1, i - 2
                if "A" in stages:
                    high_q("a", A0, a + 1)
                if "F" in stages:
                    act.wait_ge(s["o_offset_ready"], f + 1)
                    for t in range(NT):
                        ins = act.activation(o_hat[:, t, :], o[:, t, :], ACT.Identity, bias=o_offset[:, t:t + 1],
                                             scale=o_rstd[:, t:t + 1])
                    ins.then_inc(s["o_hat_ready"], 1)
                if "Z" in stages:
                    high(flat(cT["1"], HI), F0, "c_1", z + 1)
                if "A" in stages:
                    act.wait_ge(s["a_hat_ready"], a + 1)
                    act.wait_ge(s["c_a_done"], a)
                    act.copy(flat(rows_split["a"], HI), a_hat[:, :, :].rearrange("p c l -> p (c l)")).then_inc(s["rows_a_high"], 1)
                    act.wait_ge(s["v_hat_ready"], a + 1)
                    act.wait_ge(s["c_v_done"], a)
                    act.copy(flat(rows_split["v"], HI), v_hat[:, :, :].rearrange("p c l -> p (c l)")).then_inc(s["rows_v_high"], 1)
                    high_q("v", A1, a + 1)
                if "F" in stages:
                    high(halves(oT, HI, 0), F1, "oT0", f + 1)
                    high(halves(oT, HI, 1), F2, "oT1", f + 1)
                    act.wait_ge(s["ctx1_loaded"], 16 * (f + 1))
                    act.wait_ge(s["c_1_done"], f)
                    act.copy(flat(rows_split["1"], HI), ctx1_in[:, :, :].rearrange("p c l -> p (c l)")).then_inc(s["rows_1_high"], 1)
                if "A" in stages:
                    exponentials("a", A2, a + 1)
                    exponentials("v", A0, a + 1)
                if "F" in stages:
                    act.wait_ge(s["ctxT1_loaded"], 16 * (f + 1))
                    act.wait_ge(s["s_1_done"], f)
                    act.copy(flat(kT["1"], HI), ctxT1_in[:, :, :].rearrange("p c l -> p (c l)")).then_inc(s["kT_1_high"], 1)
                if "A" in stages:
                    high(flat(pT["a"], HI), A1, "pT_a", a + 1)
                    high(flat(pT["v"], HI), A2, "pT_v", a + 1)
                if "T" in stages:
                    high(halves(xT, HI, 0), N0, "xT0", n + 1)
                    high(halves(xT, HI, 1), N1, "xT1", n + 1)
                if "F" in stages:
                    high(halves(yT, HI, 0), F1, "yT0", f + 1)
                    high(halves(yT, HI, 1), F2, "yT1", f + 1)
                if "A" in stages:
                    high(flat(cT["a"], HI), A0, "c_a", a + 1)
                    high(flat(cT["v"], HI), A1, "c_v", a + 1)
                if "F" in stages:
                    high_q("1", F0, f + 1)
                    exponentials("1", F1, f + 1)
                if "T" in stages:
                    high(flat(kT["a"], HI), N0, "kT_a", n + 1)
                    high(flat(kT["v"], HI), N1, "kT_v", n + 1)
                if "F" in stages:
                    high(flat(pT["1"], HI), F2, "pT_1", f + 1)

            def fold(n, k):
                if k == "fc":
                    act.wait_ge(s["fc_loaded"], 16)
                    for j in range(ND):
                        ins = act.activation(Wfc[:, HI, j, :], raw_fc[:, j, :], ACT.Identity, scale=column("ln_g", j))
                    ins.then_inc(s["fc_high"], 1)
                    return
                if k == "fc bias":
                    return
                act.wait_ge(s["columns_loaded"], 16)
                act.wait_ge(s["vo_weights_" + k], 32)
                if k in kb:
                    act.wait_ge(s["vb_ready"], n + 1)
                if n > 0:
                    act.wait_ge(s["row_done"], n)
                for e in range(NE):
                    target = row_part[:, :] if e == 0 else row_term[:, e % 2, :]
                    if e == 3:
                        act.wait_ge(s["row_step"], STEPS * n + 1)
                    act.activation(target, raw[n % 2]["Wo"][:, e, :], ACT.Identity, scale=vbias(k)[:, e:e + 1]).then_inc(s["row_scaled"], 1)
                if k == "1":
                    act.wait_ge(s["G_done"], n + 1)
                    for j in range(2):
                        ins = act.copy(halves(M[k], HI, j), G_bank[j][:, :])
                    ins.then_inc(s["M_high"], 1)
                else:
                    act.wait_ge(s["M_scaled"], n + 1)
                    act.copy(flat(M[k], HI), M_full[:, :, :].rearrange("p c l -> p (c l)")).then_inc(s["M_high"], 1)
                act.wait_ge(s["H_done"], n + 1)
                act.wait_ge(s["O_split"], n)
                for j in range(NC):
                    if k == "1":
                        ins = act.copy(O_full[:, j, :], H_bank[j][:, :])
                    else:
                        ins = act.activation(O_full[:, j, :], H_bank[j][:, :], ACT.Identity, scale=column(k + "_g2", j))
                ins.then_inc(s["O_scaled"], 1)
                act.wait_ge(s["O_scaled"], n + 1)
                act.copy(flat(Wvo[k], HI), O_full[:, :, :].rearrange("p c l -> p (c l)")).then_inc(s["O_high"], 1)

            whole_program(act, fold, iteration)

        @block.vector
        def _(dve):
            def low(target, source, high, name, count):
                dve.wait_ge(s[name + "_high"], count)
                dve.tensor_tensor(target, source, high, ALU.subtract).then_inc(s[name + "_split"], 1)

            def low_q(k, bank, count):
                dve.wait_ge(s[f"q_{k}_high"], count)
                for j in range(NC):
                    ins = dve.scalar_tensor_tensor(out=qT[k][:, LO, j, :], in0=bank[:, j * L:(j + 1) * L],
                                                   scalar=m[k][:, j:j + 1], in1=qT[k][:, HI, j, :],
                                                   op0=ALU.add, op1=ALU.subtract)
                ins.then_inc(s[f"q_{k}_split"], 1)

            def softmax_bias(k, bank, count):
                dve.wait_ge(s[f"s_{k}_done"], count)
                dve.tensor_reduce(top[k][:, :], bank[:, :].rearrange("p (t l) -> p t l", t=NT), AX.X,
                                  ALU.max).then_inc(s["top_" + k], 1)
                dve.wait_ge(s["top_" + k], 2 * count - 1)
                dve.scalar_tensor_tensor(out=total[k][:, :], in0=top[k][:, :], scalar=SCALE, in1=shift[k][:, :],
                                         op0=ALU.mult, op1=ALU.add).then_inc(s["top_" + k], 1)
                dve.wait_ge(s["top_" + k], 2 * count)
                dve.tensor_tensor(exp_bias[k][:, :], shift[k][:, :], total[k][:, :],
                                  ALU.subtract).then_inc(s["bias_" + k], 1)

            def weigh(k, count):
                dve.wait_ge(s["exp_" + k], count)
                dve.reciprocal(inverse[k][:, :], row_sum[k][:, :]).then_inc(s["inverse_" + k], 1)
                dve.wait_ge(s["inverse_" + k], count)
                for t in range(NT):
                    ins = dve.tensor_scalar(probs[k][:, t, :], probs[k][:, t, :], inverse[k][:, t:t + 1], None, ALU.mult)
                ins.then_inc(s["probs_" + k], 1)

            def add_shift(k, source):
                for t in range(NT):
                    ins = dve.tensor_tensor_reduce(o_hat[:, t, :], source[:, t, :], u[k][:, :], SCALE, u0[k][:, 0:1],
                                                   ALU.mult, ALU.add, shift[k][:, t:t + 1])
                return ins

            def iteration(i, stages):
                n, a, f, z = i + 1, i, i - 1, i - 2
                if "A" in stages:
                    low_q("a", A0, a + 1)
                if "Z" in stages:
                    low(flat(cT["1"], LO), F0[:, :], flat(cT["1"], HI), "c_1", z + 1)
                if "N" in stages:
                    dve.wait_ge(s["ctx_loaded"], 16 * (n + 1))
                    for t in range(NK):
                        dve.bn_stats(stats[:, NT + t, :], ctx_in[:, t, :])
                    dve.wait_ge(s["fside_loaded"], 16 * (n + 1))
                    for t in range(NK):
                        dve.bn_stats(stats[:, NT + NK + t, :], fside_in[:, t, :])
                if "A" in stages:
                    low_q("v", A1, a + 1)
                if "F" in stages:
                    low(halves(oT, LO, 0), F1[:, :], halves(oT, HI, 0), "oT0", f + 1)
                    low(halves(oT, LO, 1), F2[:, :], halves(oT, HI, 1), "oT1", f + 1)
                if "N" in stages:
                    dve.wait_ge(s["x_loaded"], 16 * (n + 1))
                    for t in range(NT):
                        ins = dve.bn_stats(stats[:, t, :], x_in[:, t, :])
                    ins.then_inc(s["stats_ready"], 1)
                if "Z" in stages:
                    dve.wait_ge(s["y_bias_ready"], z + 1)
                    dve.wait_ge(s["z0_done"], z + 1)
                    dve.tensor_tensor(y[:, 0, :], N0[:, :], y[:, 0, :], ALU.add).then_inc(s["z0_ready"], 1)
                if "N" in stages:
                    dve.wait_ge(s["stats_ready"], 1)
                    dve.wait_ge(s["stats_ready"], n + 1)
                    dve.wait_ge(s["v_hat_ready"], n)
                    for j in range(NS):
                        ins = dve.bn_aggr(moments[:, j, :], stats[:, j, :])
                    ins.then_inc(s["moments_ready"], 1)
                if "N" in stages:
                    dve.wait_ge(s["moments_ready"], n + 1)
                    dve.tensor_scalar(neg_mean[:, :], moments[:, :, 0], -1.0, None, ALU.mult)
                    dve.tensor_scalar(var[:, :], moments[:, :, 1], EPS, None, ALU.add).then_inc(s["var_ready"], 1)
                if "Z" in stages:
                    dve.wait_ge(s["z1_done"], z + 1)
                    dve.tensor_tensor(y[:, 1, :], N1[:, :], y[:, 1, :], ALU.add).then_inc(s["z1_ready"], 1)
                if "A" in stages:
                    softmax_bias("a", A2, a + 1)
                    softmax_bias("v", A0, a + 1)
                    weigh("a", a + 1)
                    weigh("v", a + 1)
                if "F" in stages:
                    dve.wait_ge(s["o_bias_ready"], f + 1)
                    dve.wait_ge(s["fc0_done"], f + 1)
                    dve.wait_ge(s["out0_stored"], 16 * f)
                    dve.tensor_tensor(y[:, 0, :], F2[:, :], o[:, 0, :], ALU.add)
                if "T" in stages and "A" in stages:
                    dve.wait_ge(s["x_hat_ready"], n + 1)
                    if "F" in stages:
                        dve.wait_ge(s["shift_1"], f)
                    add_shift("a", x_hat).then_inc(s["shift_a"], 1)
                if "F" in stages:
                    dve.wait_ge(s["fc1_done"], f + 1)
                    dve.wait_ge(s["out1_stored"], 16 * f)
                    dve.tensor_tensor(y[:, 1, :], F0[:, :], o[:, 1, :], ALU.add).then_inc(s["y1_ready"], 1)
                if "A" in stages:
                    low(flat(pT["a"], LO), A1[:, :], flat(pT["a"], HI), "pT_a", a + 1)
                    low(flat(pT["v"], LO), A2[:, :], flat(pT["v"], HI), "pT_v", a + 1)
                if "T" in stages:
                    low(halves(xT, LO, 0), N0[:, :], halves(xT, HI, 0), "xT0", n + 1)
                    low(halves(xT, LO, 1), N1[:, :], halves(xT, HI, 1), "xT1", n + 1)
                if "T" in stages and "A" not in stages:
                    dve.wait_ge(s["x_hat_ready"], n + 1)
                    add_shift("a", x_hat).then_inc(s["shift_a"], 1)
                if "F" in stages:
                    low(halves(yT, LO, 0), F1[:, :], halves(yT, HI, 0), "yT0", f + 1)
                    low(halves(yT, LO, 1), F2[:, :], halves(yT, HI, 1), "yT1", f + 1)
                if "T" in stages:
                    dve.wait_ge(s["shift_a"], n + 1)
                    add_shift("v", x_hat).then_inc(s["shift_v"], 1)
                if "A" in stages:
                    low(flat(cT["a"], LO), A0[:, :], flat(cT["a"], HI), "c_a", a + 1)
                    low(flat(cT["v"], LO), A1[:, :], flat(cT["v"], HI), "c_v", a + 1)
                if "F" in stages:
                    dve.wait_ge(s["y1_ready"], f + 1)
                    if "N" in stages:
                        dve.wait_ge(s["shift_v"], n + 1)
                    add_shift("1", y).then_inc(s["shift_1"], 1)
                    low_q("1", F0, f + 1)
                if "A" in stages:
                    dve.wait_ge(s["x_bias_ready"], a + 1)
                    dve.wait_ge(s["attn0_done"], a + 1)
                    dve.tensor_tensor(o[:, 0, :], A2[:, :], x_bias[:, 0, :], ALU.add).then_inc(s["o0_ready"], 1)
                if "F" in stages:
                    dve.wait_ge(s["shift_1"], f + 1)
                    softmax_bias("1", F1, f + 1)
                if "A" in stages:
                    dve.wait_ge(s["o0_ready"], a + 1)
                    dve.bn_stats(o_stats[:, 0, :], o[:, 0, :])
                if "F" in stages:
                    weigh("1", f + 1)
                if "A" in stages:
                    dve.wait_ge(s["attn1_done"], a + 1)
                    dve.tensor_tensor(o[:, 1, :], A1[:, :], x_bias[:, 1, :], ALU.add).then_inc(s["o1_ready"], 1)
                    dve.wait_ge(s["o1_ready"], a + 1)
                    dve.bn_stats(o_stats[:, 1, :], o[:, 1, :]).then_inc(s["o_stats_ready"], 1)
                    dve.wait_ge(s["o_stats_ready"], 1)
                    dve.wait_ge(s["o_stats_ready"], a + 1)
                    for t in range(NT):
                        ins = dve.bn_aggr(o_moments[:, t, :], o_stats[:, t, :])
                    ins.then_inc(s["o_moments_ready"], 1)
                    dve.wait_ge(s["o_moments_ready"], a + 1)
                    dve.tensor_scalar(o_neg_mean[:, :], o_moments[:, :, 0], -1.0, None, ALU.mult)
                    dve.tensor_scalar(o_var[:, :], o_moments[:, :, 1], EPS, None, ALU.add).then_inc(s["o_var_ready"], 1)
                if "F" in stages:
                    low(flat(pT["1"], LO), F2[:, :], flat(pT["1"], HI), "pT_1", f + 1)
                if "T" in stages:
                    low(flat(kT["a"], LO), N0[:, :], flat(kT["a"], HI), "kT_a", n + 1)
                    low(flat(kT["v"], LO), N1[:, :], flat(kT["v"], HI), "kT_v", n + 1)

            def fold(n, k):
                if k == "fc":
                    dve.wait_ge(s["columns_loaded"], 16)
                    dve.wait_ge(s["fc_high"], 1)
                    for j in range(ND):
                        ins = dve.scalar_tensor_tensor(out=Wfc[:, LO, j, :], in0=raw_fc[:, j, :], scalar=column("ln_g", j),
                                                       in1=Wfc[:, HI, j, :], op0=ALU.mult, op1=ALU.subtract)
                    ins.then_inc(s["fc_split"], 1)
                    return
                if k == "fc bias":
                    dve.wait_ge(s["row_done"], 4)
                    dve.tensor_tensor(bias_fc[:, :], fc_row_bank[:, :], bias_fc[:, :], ALU.add).then_inc(s["row_copied"], 1)
                    return
                normed = k in kb
                w = raw[n % 2]
                if n == 0:
                    dve.wait_ge(s["Wq_rest_loaded"], 16)
                dve.wait_ge(s["columns_loaded"], 16)
                dve.wait_ge(s["qk_weights_" + k], 32)

                def sums(target, matrix, vector, first, chunks, done):
                    width = vector.shape[-1]
                    for j, e in enumerate(chunks):
                        term = terms[:, j * width // 256:(j + 1) * width // 256, :].rearrange("p a b -> p (a b)")
                        ins = dve.tensor_tensor_reduce(term, matrix[:, e, :], vector[:, :], 1.0, first[:, e:e + 1],
                                                       ALU.mult, ALU.add, target[:, e:e + 1])
                    ins.then_inc(s[done], 1)
                    dve.wait_ge(s[done], n + 1)

                if normed:
                    dve.wait_ge(s[f"rows_{k}_loaded"], 64)
                    sums(kb[k], w["WkT"], row[k + "_b2"], column(k + "_bk"), range(NE), "kb_ready")
                    sums(qb[k], w["WqT"], row[k + "_b1"], column(k + "_bq"), (0, 1), "qb_half")
                    sums(qb[k], w["WqT"], row[k + "_b1"], column(k + "_bq"), (2, 3), "qb_ready")
                    dve.wait_ge(s["vo_weights_" + k], 32)
                    sums(vb[k], w["WvT"], row[k + "_b2"], column(k + "_bv"), range(NE), "vb_ready")
                dve.tensor_tensor_reduce(terms[:, 0, 0:NE], qbias(k)[:, :], kbias(k)[:, :], 1.0, 0.0,
                                         ALU.mult, ALU.add, qk[k][:, :]).then_inc(s["qk_ready"], 1)
                dve.wait_ge(s["qk_ready"], n + 1)
                dve.wait_ge(s["u_done"], n)
                dve.tensor_scalar(u_part[:, :], w["WqT"][:, 0, :], kbias(k)[:, 0:1], None,
                                  ALU.mult).then_inc(s["u_step"], 1)
                for e in range(1, NE):
                    dve.wait_ge(s["u_step"], NE * n + e)
                    ins = dve.scalar_tensor_tensor(out=u_part[:, :], in0=w["WqT"][:, e, :], scalar=kbias(k)[:, e:e + 1],
                                                   in1=u_part[:, :], op0=ALU.mult, op1=ALU.add)
                    ins.then_inc(s["u_step"], 1)
                dve.wait_ge(s["G_done"], n + 1)
                if normed:
                    for j in range(ND):
                        ins = dve.scalar_tensor_tensor(
                            out=M_full[:, j, :], in0=G_bank[j // 2][:, (j % 2) * C:(j % 2 + 1) * C],
                            scalar=column(k + "_g1", j), in1=row[k + "_g2"][:, :], op0=ALU.mult, op1=ALU.mult)
                    ins.then_inc(s["M_scaled"], 1)
                    dve.wait_ge(s["M_high"], n + 1)
                    dve.tensor_tensor(flat(M[k], LO), M_full[:, :, :].rearrange("p c l -> p (c l)"), flat(M[k], HI),
                                      ALU.subtract).then_inc(s["M_split"], 1)
                else:
                    dve.wait_ge(s["M_high"], n + 1)
                    for j in range(2):
                        ins = dve.tensor_tensor(halves(M[k], LO, j), G_bank[j][:, :], halves(M[k], HI, j), ALU.subtract)
                    ins.then_inc(s["M_split"], 1)
                dve.wait_ge(s["M_split"], n + 1)
                dve.wait_ge(s["u_done"], n + 1)
                if normed:
                    dve.tensor_tensor(u[k][:, :], u_bank[:, :], u[k][:, :], ALU.mult).then_inc(s["u_copied"], 1)
                else:
                    dve.tensor_copy(u[k][:, :], u_bank[:, :]).then_inc(s["u_copied"], 1)
                dve.wait_ge(s["m_done"], n + 1)
                if normed:
                    dve.tensor_tensor(m[k][:, :], small_bank[:, 0:NC], column(k + "_g2"), ALU.mult)
                else:
                    dve.tensor_copy(m[k][:, :], small_bank[:, 0:NC])
                dve.tensor_scalar(u0[k][:, :], small_bank[:, NC:NC + 1], SCALE, None, ALU.mult).then_inc(s["m_copied"], 1)
                if k != "a":
                    dve.wait_ge(s["biases_loaded"], 64)
                    bias = bias_attn if k == "v" else bias_1
                    if k == "v":
                        dve.tensor_tensor(bias[:, :], bias[:, :], row["v_bo"][:, :], ALU.add).then_inc(s["row_added"], 1)
                        dve.wait_ge(s["row_added"], 1)
                    dve.wait_ge(s["row_done"], n + 1)
                    dve.tensor_tensor(bias[:, :], row_bank[k][:, :], bias[:, :], ALU.add).then_inc(s["row_copied"], 1)
                dve.wait_ge(s["O_high"], n + 1)
                dve.tensor_tensor(flat(Wvo[k], LO), O_full[:, :, :].rearrange("p c l -> p (c l)"), flat(Wvo[k], HI),
                                  ALU.subtract).then_inc(s["O_split"], 1)

            whole_program(dve, fold, iteration)

        @block.gpsimd
        def _(pool):
            pool.memset(ones[:, :], 1.0).then_inc(s["ones_ready"], 1)
            pool.memset(ident[:, :], 0.0).then_inc(s["ident_ready"], 1)
            pool.wait_ge(s["ident_ready"], 1)
            pool.affine_select(out=ident[:, :], in_=ident[:, :], compare_op=ALU.not_equal, fill=1.0, base=0,
                               pattern=[[-1, P]], channel_multiplier=1).then_inc(s["ident_ready"], 1)
            pool.memset(power[:, :], -0.5).then_inc(s["power_set"], 1)
            pool.wait_ge(s["power_set"], 1)

            def normalise(target, source, scale, shift, t):
                return pool.tensor_scalar(target[:, t, :], source[:, t, :], scale, shift, ALU.mult, ALU.add)

            def low(target, source, high, name, count):
                pool.wait_ge(s[name + "_high"], count)
                pool.tensor_tensor(target, source, high, ALU.subtract).then_inc(s[name + "_split"], 1)

            def iteration(i, stages):
                n, a, f, z = i + 1, i, i - 1, i - 2
                if "F" in stages:
                    pool.wait_ge(s["o_var_ready"], f + 1)
                    pool.tensor_tensor(o_rstd[:, :], o_var[:, :], power[:, 0:NT], ALU.pow).then_inc(s["o_rstd_ready"], 1)
                    pool.wait_ge(s["o_rstd_ready"], f + 1)
                    pool.tensor_tensor(o_offset[:, :], o_neg_mean[:, :], o_rstd[:, :], ALU.mult).then_inc(s["o_offset_ready"], 1)
                if "A" in stages:
                    pool.wait_ge(s["x_loaded"], 16 * (a + 1))
                    pool.wait_ge(s["o1_ready"], a)
                    for t in range(NT):
                        ins = pool.tensor_tensor(x_bias[:, t, :], x_in[:, t, :], bias_attn[:, :], ALU.add)
                    ins.then_inc(s["x_bias_ready"], 1)
                    low(flat(rows_split["a"], LO), a_hat[:, :, :].rearrange("p c l -> p (c l)"), flat(rows_split["a"], HI), "rows_a", a + 1)
                    low(flat(rows_split["v"], LO), v_hat[:, :, :].rearrange("p c l -> p (c l)"), flat(rows_split["v"], HI), "rows_v", a + 1)
                if "F" in stages:
                    pool.wait_ge(s["o_hat_ready"], f + 1)
                    pool.wait_ge(s["row_copied"], 3)
                    for t in range(NT):
                        ins = pool.tensor_tensor(o[:, t, :], o[:, t, :], bias_fc[:, :], ALU.add)
                    ins.then_inc(s["o_bias_ready"], 1)
                    low(flat(rows_split["1"], LO), ctx1_in[:, :, :].rearrange("p c l -> p (c l)"), flat(rows_split["1"], HI), "rows_1", f + 1)
                if "T" in stages:
                    pool.wait_ge(s["var_ready"], n + 1)
                    pool.tensor_tensor(rstd[:, :], var[:, :], power[:, :], ALU.pow).then_inc(s["rstd_ready"], 1)
                    pool.wait_ge(s["rstd_ready"], n + 1)
                    pool.tensor_tensor(offset[:, :], neg_mean[:, :], rstd[:, :], ALU.mult).then_inc(s["offset_ready"], 1)
                    pool.wait_ge(s["power_set"], 1)
                    pool.wait_ge(s["offset_ready"], n + 1)
                    pool.wait_ge(s["xT1_done"], n)
                    pool.wait_ge(s["shift_v"], n)
                    for t in range(NT):
                        ins = normalise(x_hat, x_in, rstd[:, t:t + 1], offset[:, t:t + 1], t)
                    ins.then_inc(s["x_hat_ready"], 1)
                    pool.wait_ge(s["power_set"], 1)
                    pool.wait_ge(s["rows_a_split"], n)
                    pool.wait_ge(s["kT_a_done"], n)
                    for t in range(NK):
                        ins = normalise(a_hat, ctx_in, rstd[:, NT + t:NT + t + 1], offset[:, NT + t:NT + t + 1], t)
                    ins.then_inc(s["a_hat_ready"], 1)
                    pool.wait_ge(s["power_set"], 1)
                    pool.wait_ge(s["rows_v_split"], n)
                    pool.wait_ge(s["kT_v_done"], n)
                    for t in range(NK):
                        ins = normalise(v_hat, fside_in, rstd[:, NT + NK + t:NT + NK + t + 1],
                                        offset[:, NT + NK + t:NT + NK + t + 1], t)
                    ins.then_inc(s["v_hat_ready"], 1)
                if "F" in stages:
                    low(flat(kT["1"], LO), ctxT1_in[:, :, :].rearrange("p c l -> p (c l)"), flat(kT["1"], HI), "kT_1", f + 1)
                    pool.wait_ge(s["yT1_done"], f + 1)
                    pool.wait_ge(s["shift_1"], f + 1)
                    for t in range(NT):
                        ins = pool.tensor_tensor(y[:, t, :], y[:, t, :], bias_1[:, :], ALU.add)
                    ins.then_inc(s["y_bias_ready"], 1)

            def weighted_sum(part, term, matrix, vector, before, step):
                def times(target, e):
                    column_e = vector[:, e:e + 1].to_broadcast([P, matrix.shape[-1]])
                    return pool.tensor_tensor(target, matrix[:, e, :], column_e, ALU.mult)

                times(part, 0)
                for e in range(1, NE):
                    times(term, e).then_inc(s[step], 1)
                    pool.wait_ge(s[step], before + 2 * e - 1)
                    pool.tensor_tensor(part, part, term, ALU.add).then_inc(s[step], 1)
                    pool.wait_ge(s[step], before + 2 * e)

            def fold(n, k):
                if k == "fc":
                    return
                if k == "fc bias":
                    pool.wait_ge(s["fc_loaded"], 16)
                    weighted_sum(row_part[:, :], row_term[:, 0, :], raw_fc, column("ln_b"), 0, "fc_row_step")
                    return
                pool.wait_ge(s["columns_loaded"], 16)
                pool.wait_ge(s["qk_weights_" + k], 32)
                if k in kb:
                    pool.wait_ge(s["qb_ready"], n + 1)
                if n > 0:
                    pool.wait_ge(s["m_done"], n)
                weighted_sum(m_part[:, :], m_term[:, :], raw[n % 2]["WkT"], qbias(k), SUM_STEPS * n, "m_step")
                for e in range(1, NE):
                    if e > 1:
                        pool.wait_ge(s["row_step"], STEPS * n + e - 1)
                    pool.wait_ge(s["row_scaled"], NE * n + e + 1)
                    pool.tensor_tensor(row_part[:, :], row_part[:, :], row_term[:, e % 2, :], ALU.add).then_inc(s["row_step"], 1)

            def folded():
                pool.wait_ge(s["row_done"], 3)
                pool.wait_ge(s["M_split"], 3)
                pool.wait_ge(s["O_split"], 3)

            whole_program(pool, fold, iteration, folded)


def kernel(**inputs):
    import numpy as np
    import concourse.bacc as bacc
    from concourse.bass_utils import run_bass_kernel_spmd

    nc = bacc.Bacc("TRN2", target_bir_lowering=False, num_devices=1)
    arrays = {}

    def dram(name, a):
        arrays[name] = np.ascontiguousarray(a)
        return nc.dram_tensor(name, arrays[name].shape, mybir.dt.from_np(arrays[name].dtype), kind="ExternalInput").ap()

    prefix = {"a": "L0_xattn_a_", "v": "L0_xattn_v_", "1": "L1_xattn_"}
    source = {"ln1_g": "g1", "ln1_b": "b1", "ln2_g": "g2", "ln2_b": "b2"}
    named = {f"{k}_{source.get(name, name)}": np.asarray(inputs[prefix[k] + name])
             for k in "av1" for name in (*source, "bq", "bk", "bv", "bo") if prefix[k] + name in inputs}
    named |= {name: np.asarray(inputs["L0_xattn_" + name]) for name in ("ln_g", "ln_b", "fc_b")}

    vectors = dram("vectors", np.concatenate([named[n].reshape(-1, P).T for n, _ in VECTORS], axis=1))
    rows = {n: dram("row_" + n, named[n]) for n, _ in ROWS}
    weights = {}
    for k in "av1":
        Wq, Wk, Wv, Wo = (np.asarray(inputs[prefix[k] + n]) for n in ("Wq", "Wk", "Wv", "Wo"))
        own = {"WqT": Wq.T, "WkT": Wk.T, "WvT": Wv.T, "Wo": Wo}
        weights[k] = {n: dram(f"{n}_{k}", w) for n, w in own.items()}
    x = dram("x", inputs["x"])
    ctx = dram("ctx", inputs["ctx_512"])
    ctxT = dram("ctxT", np.asarray(inputs["ctx_512"]).transpose(0, 2, 1))
    fside = dram("fside", inputs["fside_BxSxS_0"])
    fc_W = dram("fc_W", inputs["L0_xattn_fc_W"])
    out = nc.dram_tensor("out", x.shape, F32, kind="ExternalOutput").ap()
    build_kernel(nc, x, ctx, ctxT, fside, vectors, rows, weights, fc_W, out)
    result = run_bass_kernel_spmd(nc, [arrays], core_ids=[0])
    return result.results[0]["out"]
```
